# Optimizing a Trainium2 kernel written in Bass

```python
import numpy as np
import jax
import jax.numpy as jnp

def _softmax(x, axis=-1):
    return jax.nn.softmax(x, axis=axis)

def _gelu(x):
    return jax.nn.gelu(x, approximate=True)

def _silu(x):
    return jax.nn.silu(x)

def _sigmoid(x):
    return jax.nn.sigmoid(x)

def _layernorm(x, axis=-1, eps=1e-05):
    m = jnp.mean(x, axis=axis, keepdims=True)
    v = jnp.var(x, axis=axis, keepdims=True)
    return (x - m) / jnp.sqrt(v + eps)

def _scatter_add(tgt, idx, src, axis=0):
    return tgt.at[idx].add(src)

def _segment_sum(src, seg, n):
    return jax.ops.segment_sum(src, seg, n)
kernel_name = 'mk_seq_preln_d1_jaxref_r4_6cd3c4'

def setup_inputs(seed: int=0):
    np.random.seed(seed)
    _w = jnp.asarray

    def _L0_attn_setup():
        import jax, jax.numpy as jnp
        import numpy as np
        D_MODEL = 512
        N_QUERY = 4
        N_HEAD = 8
        D_HEAD = D_MODEL // (N_QUERY * N_HEAD)
        D_KV = D_HEAD * N_HEAD
        BATCH, SEQ = (2, 512)
        key = jax.random.key(seed)
        ks = jax.random.split(key, 5)
        w_scale = 1.0 / np.sqrt(D_MODEL).astype(np.float32)
        x = jax.random.normal(ks[0], (BATCH, SEQ, D_MODEL), jnp.float32)
        Wq = jax.random.normal(ks[1], (D_MODEL, D_MODEL), jnp.float32) * w_scale
        Wk = jax.random.normal(ks[2], (D_KV, D_MODEL), jnp.float32) * w_scale
        Wv = jax.random.normal(ks[3], (D_KV, D_MODEL), jnp.float32) * w_scale
        memory = jax.random.normal(ks[4], (D_KV, D_KV), jnp.float32) * 0.02
        memory_norm = jnp.ones((D_KV, 1), jnp.float32)
        memory_weight = jnp.ones((1,), jnp.float32)
        return dict(x=x, Wq=Wq, Wk=Wk, Wv=Wv, memory=memory, memory_norm=memory_norm, memory_weight=memory_weight)
    _L0_attn_in = _L0_attn_setup()

    def _L0_ffn_setup():
        import jax, jax.numpy as jnp
        import numpy as np
        _FP8_DTYPE = jnp.float8_e4m3fn
        _FP8_MAX = 448.0
        key = jax.random.key(seed)
        k_x, k_w = jax.random.split(key)
        B, S, IN, OUT = (2, 2048, 512, 512)
        x = jax.random.normal(k_x, (B, S, IN), dtype=jnp.float32)
        w_f32 = jax.random.normal(k_w, (OUT, IN), dtype=jnp.float32) * 0.02
        weight = w_f32.astype(_FP8_DTYPE)
        weight_scale = jnp.asarray(1.5, dtype=jnp.float32)
        input_scale = jnp.asarray(0.75, dtype=jnp.bfloat16)
        return {'x': x, 'weight': weight, 'weight_scale': weight_scale, 'input_scale': input_scale}
    _L0_ffn_in = _L0_ffn_setup()
    _d = {'L0_attn_x': _L0_attn_in['x'], 'L0_attn_Wq': _L0_attn_in['Wq'], 'L0_attn_Wk': _L0_attn_in['Wk'], 'L0_attn_Wv': _L0_attn_in['Wv'], 'L0_attn_memory': _L0_attn_in['memory'], 'L0_attn_memory_norm': _L0_attn_in['memory_norm'], 'L0_attn_memory_weight': _L0_attn_in['memory_weight'], 'L0_ffn_weight': _L0_ffn_in['weight'], 'L0_ffn_weight_scale': _L0_ffn_in['weight_scale'], 'L0_ffn_input_scale': _L0_ffn_in['input_scale']}
    _x0 = _d['L0_attn_x']
    _d['L0_attn_x'] = jax.random.normal(jax.random.fold_in(jax.random.key(seed), 1), (2, 2048, 512), dtype=_x0.dtype)
    del _x0
    return _d

def reference(L0_attn_x, L0_attn_Wq, L0_attn_Wk, L0_attn_Wv, L0_attn_memory, L0_attn_memory_norm, L0_attn_memory_weight, L0_ffn_weight, L0_ffn_weight_scale, L0_ffn_input_scale):

    def _L0_attn_ref(x, Wq, Wk, Wv, memory, memory_norm, memory_weight):
        import jax, jax.numpy as jnp
        import numpy as np
        D_MODEL = 512
        N_QUERY = 4
        N_HEAD = 8
        D_HEAD = D_MODEL // (N_QUERY * N_HEAD)
        D_KV = D_HEAD * N_HEAD
        BATCH, SEQ = (2, 512)
        b, s, d = x.shape
        q = x @ Wq.T
        k = x @ Wk.T
        v = x @ Wv.T
        qh = q.reshape(b, s, N_QUERY, N_HEAD, D_HEAD)
        kh = k.reshape(b, s, N_HEAD, D_HEAD)
        vh = v.reshape(b, s, N_HEAD, D_HEAD)
        scale = np.float32(1.0 / np.sqrt(np.float32(D_HEAD)))
        scores = jnp.einsum('bsqhd,bthd->bqhst', qh, kh) * scale
        probs = jax.nn.softmax(scores, axis=-1)
        a_dot = jnp.einsum('bqhst,bthd->bsqhd', probs, vh)
        a_dot = a_dot.reshape(b, s, N_QUERY * N_HEAD, D_HEAD)
        sigma_q = jax.nn.elu(q.reshape(b, s, N_QUERY, D_KV))
        a_mem = sigma_q @ memory / (sigma_q @ memory_norm)
        a_mem = a_mem.reshape(b, s, N_QUERY * N_HEAD, D_HEAD)
        w = jax.nn.sigmoid(memory_weight)
        out = a_dot * (1.0 - w) + a_mem * w
        return out.reshape(b, s, D_MODEL)

    def _L0_ffn_ref(x, weight, weight_scale, input_scale):
        import jax, jax.numpy as jnp
        import numpy as np
        _FP8_DTYPE = jnp.float8_e4m3fn
        _FP8_MAX = 448.0
        orig_dtype = x.dtype
        w = weight.astype(orig_dtype) * weight_scale.astype(orig_dtype)
        s_f32 = input_scale.astype(jnp.float32)
        x_scaled = x.astype(jnp.float32) / s_f32
        x_fp8 = jnp.clip(x_scaled, -_FP8_MAX, _FP8_MAX).astype(_FP8_DTYPE)
        x_qdq = x_fp8.astype(orig_dtype) * s_f32.astype(orig_dtype)
        return jnp.einsum('bsi,oi->bso', x_qdq, w)
    x = L0_attn_x
    x = x + _L0_attn_ref(_layernorm(x, axis=-1), L0_attn_Wq, L0_attn_Wk, L0_attn_Wv, L0_attn_memory, L0_attn_memory_norm, L0_attn_memory_weight)
    x = x + _L0_ffn_ref(_layernorm(x, axis=-1), L0_ffn_weight, L0_ffn_weight_scale, L0_ffn_input_scale)
    return x

_drawn_inputs = setup_inputs


def setup_inputs(seed=0):
    import zlib

    import numpy as np

    out = dict(_drawn_inputs(seed))
    spreads = {'L0_attn_memory_norm': (1.0, 0.2)}
    factors = {'L0_attn_Wk': 2.805, 'L0_attn_Wv': 2.705}
    for name, (base, spread) in spreads.items():
        noise = np.random.default_rng([zlib.crc32(name.encode()), seed]).standard_normal(out[name].shape)
        drawn = base * np.exp(spread * noise) if base else spread * noise
        out[name] = jnp.asarray(drawn.astype(out[name].dtype))
    for name, factor in factors.items():
        out[name] = (out[name] * factor).astype(out[name].dtype)
    return out
```

```python
from contextlib import ExitStack

import concourse.bass as bass
import numpy as np
from concourse import mybir
from concourse.alu_op_type import AluOpType as ALU

F32 = mybir.dt.float32
BF16 = mybir.dt.bfloat16
I32 = mybir.dt.int32
U8 = mybir.dt.uint8
ACT = mybir.ActivationFunctionType
AX = mybir.AxisListType
MAX_OVER_PARTITIONS = bass.bass_isa.ReduceOp.max

P = 128
BATCH, SEQ, DM = 2, 2048, 512
HEADS, QG, DH = 8, 4, 16
KV = HEADS * DH
CH = 512
CPB = SEQ // CH
NG = BATCH * CPB
TPC = CH // P
KT = DM // P
NT = NG * TPC
ST = SEQ // P
VW = 32
SPLIT = 3
Q_PART = (0, 0, 0, 1, 1, 2)
K_PART = (0, 1, 2, 0, 1, 0)
TERMS = len(Q_PART)
ROWS = TERMS * DH
AUG = ROWS + SPLIT
SCALE = DH ** -0.5
LN_EPS = 1e-5
FP8_MAX = 448.0
ONE_FREE, TWO_FREE = 1, 2
STRIPS = QG * ST
UNIT = 3
UNITS = -(-STRIPS // UNIT)
SLOTS = 2
PSLOTS = 4
GUARD_MARGIN = 1.02
GUARD_LIMIT = 130.0 / (SCALE * GUARD_MARGIN)
GUARD_OFFSET = 3.0 / SCALE
TURN_AT = 5
FFN_AT = (8, 9, 11, 12, 14, 15, 17, 18)


def strips(unit):
    return range(UNIT * unit, min(UNIT * unit + UNIT, STRIPS))


def attention_ffn(nc, x, Wq, Wk, Wv, memory, memory_norm, memory_weight, weight, weight_scale, input_scale, out,
                  q_aug, k_aug, v_aug, guard):
    x_tiles = x.rearrange("(t p) d -> p t d", p=P)
    out_tiles = out.rearrange("(t p) d -> p t d", p=P)

    with ExitStack() as ctx:
        def sb(name, shape, dt):
            return ctx.enter_context(nc.sbuf_tensor(name, shape, dt))

        def sem(name):
            return ctx.enter_context(nc.semaphore(name))

        ps = ctx.enter_context(nc.psum_tensor("ps", [P, 8, 512], F32))

        resid = sb("resid", [P, NT, DM], F32)
        ident = sb("ident", [P, P], F32)
        ident_bf = sb("ident_bf", [P, P], BF16)
        head_ones = sb("head_ones", [P, P], BF16)
        minus_half = sb("minus_half", [P, TPC], F32)
        eps = sb("eps", [P, TPC], F32)
        half = sb("half", [P, 2 * BATCH], F32)
        k_sum = sb("k_sum", [P, NG], F32)
        k_total = sb("k_total", [P, BATCH], F32)
        k_mean_sq = sb("k_mean_sq", [P, BATCH], BF16)
        wT_ffn = sb("wT_ffn", [P, KT, DM], BF16)
        scalars = sb("scalars", [P, 10], F32)
        mem_w, e_neg, one_plus, w_mem, w_dot, ws_col, s_col, inv_s, sw = (scalars[:, i:i + 1] for i in range(9))
        s_raw = sb("s_raw", [P, 1], BF16)
        q_st = sb("q_st", [P, 2, QG * CH], BF16)
        k_st = sb("k_st", [P, 2, SEQ], BF16)
        v_st = sb("v_st", [P, 2, ST, VW], F32)
        pool = sb("pool", [P, 8192], F32)
        probs = pool[:, 0:PSLOTS * UNIT * CH].rearrange("p (a b) -> p a b", a=PSLOTS)
        oT = sb("oT", [P, 2, CH], F32)
        rden = sb("rden", [P, TPC, QG], F32)
        head_out = sb("head_out", [P, TPC, QG, DH], F32)
        xnT = pool[:, 0:4096].rearrange("p (a k s) -> p a k s", a=2, k=KT)
        xn = pool[:, 4096:6144].rearrange("p (t d) -> p t d", t=TPC)
        sigma = pool[:, 6144:8192].rearrange("p (o s) -> p o s", o=QG)
        wqT = sb("wqT", [P, KT, DM], F32)
        wkT = sb("wkT", [P, KT, KV], F32)
        wvT = sb("wvT", [P, KT, KV], F32)
        mem_aug = sb("mem_aug", [P, KV + 1], F32)
        parts = sb("parts", [P, QG + 1, SPLIT, CH], BF16)
        sq = sb("sq", [P, 2, CH], BF16)
        v_tiles = sb("v_tiles", [P, 2, HEADS, TPC, VW], F32)
        work = sb("work", [P, 10, CH], F32)
        p32, r32, neg, epos, relu = (work[:, 2 * i:2 * i + 2, :] for i in range(5))
        y_out = sb("y_out", [P, TPC, DM], F32)
        wq_raw = y_out
        wkv_raw = sb("wkv_raw", [P, 2, DM], F32)
        xq = wkv_raw[:, :, :].bitcast(BF16).rearrange("p a (b d) -> p (a b) d", b=2)
        w8 = sb("w8", [P, KT, DM], mybir.dt.float8e4)
        w_val = sb("w_val", [P, KT, DM], BF16)
        xqT = sb("xqT", [P, KT, P], BF16)
        stats = sb("stats", [P, TPC, 6], F32)
        moments = sb("moments", [P, 2, TPC, 2], F32)
        var_eps = sb("var_eps", [P, TPC], F32)
        rstd = sb("rstd", [P, 2, TPC], F32)
        rstd_s = sb("rstd_s", [P, TPC], F32)
        rnorm = sb("rnorm", [P, 2, 2], F32)
        norm2 = sb("norm2", [P, NG, QG + 1], F32)
        bound = sb("bound", [P, 9, BATCH], F32)
        range_all = sb("range_all", [P, BATCH], F32)
        widest = sb("widest", [P, 1], F32)
        guard_rest = sb("guard_rest", [P, BATCH], F32)
        guard_parts = sb("guard_parts", [P, BATCH, SPLIT], F32)
        guard_bf = sb("guard_bf", [P, BATCH, SPLIT], BF16)
        ones_row = sb("ones_row", [P, CH], BF16)
        guard_rows = wqT[:, :, :].rearrange("p k o -> p (k o)").bitcast(BF16)[:, 0:BATCH * SPLIT * CH]\
            .rearrange("p (b i s) -> p b i s", b=BATCH, i=SPLIT)
        wide = sb("wide", [P, 1], I32)
        row_max = sb("row_max", [P, QG * TPC], F32)
        gm_rest = sb("gm_rest", [QG * TPC, P], F32)
        gm_parts = sb("gm_parts", [QG * TPC, SPLIT, P], BF16)

        tp = [ps[:, i, :] for i in (0, 1)]
        pj = [ps[:, i, :] for i in (2, 3)]
        vp = ps[:, 4, :]
        am = [ps[:, i, 0:2 * (KV + 1)].rearrange("p (q c) -> p q c", q=2) for i in (5, 6)]
        n2 = ps[:, 7, :]
        sc = [ps[:, UNIT * i:UNIT * i + UNIT, :] for i in range(SLOTS)]
        acc = [ps[:, i, :] for i in (6, 7)]
        tr = [a.rearrange("p (t q r) -> p t q r", t=TPC, q=QG) for a in acc]
        ffn_ps = acc[0]
        ffn_tp = acc[0][:, 0:CH // 2].bitcast(BF16)
        ffn_wtp = acc[1][:, 0:CH // 2].bitcast(BF16)

        x_loaded = [sem(f"x_loaded{i}") for i in range(2)]
        w_loaded = sem("w_loaded")
        small_loaded = sem("small_loaded")
        w8_loaded = sem("w8_loaded")
        zeros_set = sem("zeros_set")
        consts_set = sem("consts_set")
        ones_set = sem("ones_set")
        e_neg_ready = sem("e_neg_ready")
        scal = sem("scal")
        w_turned = sem("w_turned")
        w_copied = sem("w_copied")
        dec = sem("dec")
        wf_turned = sem("wf_turned")
        wf_copied = sem("wf_copied")
        stats_ready = sem("stats_ready")
        moments_ready = sem("moments_ready")
        eps_added = sem("eps_added")
        rstd_ready = sem("rstd_ready")
        xn_ready = sem("xn_ready")
        tp_ready = sem("tp_ready")
        xnT_ready = sem("xnT_ready")
        proj_ready = sem("proj_ready")
        p32_ready = sem("p32_ready")
        part1_ready = sem("part1_ready")
        rest_ready = sem("rest_ready")
        part2_ready = sem("part2_ready")
        part3_ready = sem("part3_ready")
        parts_stored = [sem(f"parts_stored{i}") for i in range(QG + 1)]
        neg_ready = sem("neg_ready")
        relu_ready = sem("relu_ready")
        epos_ready = sem("epos_ready")
        sigma_ready = sem("sigma_ready")
        sq_ready = sem("sq_ready")
        n2_ready = sem("n2_ready")
        v_proj_ready = sem("v_proj_ready")
        v_tile_ready = sem("v_tile_ready")
        v_stored = [sem(f"v_stored{i}") for i in range(2)]
        am_ready = sem("am_ready")
        am_used = sem("am_used")
        n2_used = sem("n2_used")
        rnorm_ready = sem("rnorm_ready")
        gd = sem("gd")
        bound_in = sem("bound_in")
        k_mean_ready = sem("k_mean_ready")
        k_mean_norm = sem("k_mean_norm")
        bound_root = sem("bound_root")
        range_ready = sem("range_ready")
        bound_all = sem("bound_all")
        guard_rows_ready = sem("guard_rows_ready")
        wide_ready = sem("wide_ready")
        guard_stored = sem("guard_stored")
        gm_loaded = sem("gm_loaded")
        gm_scores = sem("gm_scores")
        gm_scores_used = sem("gm_scores_used")
        gm_turned = sem("gm_turned")
        gm_step = sem("gm_step")
        gm_split = sem("gm_split")
        gm_stored = sem("gm_stored")
        operands_loaded = [sem(f"operands_loaded{i}") for i in range(2)]
        scores_ready = sem("scores_ready")
        probs_ready = sem("probs_ready")
        pv_done = sem("pv_done")
        oT_ready = sem("oT_ready")
        tr_ready = sem("tr_ready")
        rden_ready = sem("rden_ready")
        head_out_ready = sem("head_out_ready")
        f_moments = sem("f_moments")
        f_eps = sem("f_eps")
        f_rstd = sem("f_rstd")
        f_step = sem("f_step")
        xq_ready = sem("xq_ready")
        xq_turned = sem("xq_turned")
        xqT_ready = sem("xqT_ready")
        ffn_ready = sem("ffn_ready")
        y_ready = sem("y_ready")
        y_stored = sem("y_stored")

        block = ctx.enter_context(nc.Block())

        @block.sync
        def _(sp):
            def load_x(c, par):
                sp.dma_start(resid[:, bass.ds(c * TPC, TPC), :], x_tiles[:, bass.ds(c * TPC, TPC), :])\
                    .then_inc(x_loaded[par], 16)

            for o in range(QG + 1):
                sp.sem_inc(parts_stored[o], 16 * TERMS)
            for par in range(2):
                sp.sem_inc(v_stored[par], 16)
            sp.sem_inc(y_stored, 16)
            sp.sem_inc(gm_stored, 16)

            load_x(0, 0)
            load_x(1, 1)
            sp.dma_start(w8[:, :, :], weight.rearrange("(a p) i -> p a i", p=P)).then_inc(w8_loaded, 16)

            def store_parts(c, it, last):
                for par in range(2):
                    if not last:
                        sp.wait_ge(x_loaded[par], 16 * it + 16)
                        load_x(c + par + 2, par)
                    for o in range(QG + 1):
                        sp.wait_ge(part3_ready, (c + par) * (QG + 1) + o + 1)
                        for r in range(TERMS):
                            rows = slice(r * DH, r * DH + DH)
                            if o < QG:
                                dst = q_aug[bass.ds((c + par) * HEADS, HEADS), rows, o * CH:o * CH + CH]
                                src = parts[:, o, Q_PART[r], :]
                            else:
                                dst = k_aug[bass.ds((c + par) * HEADS, HEADS), rows, :]
                                src = parts[:, o, K_PART[r], :]
                            sp.dma_start(dst, src).then_inc(parts_stored[o], 16)
                    sp.wait_ge(v_tile_ready, c + par + 1 + ONE_FREE)
                    sp.dma_start(v_dst(c + par), v_tiles[:, par, :, :, :].rearrange("p h t w -> p h (t w)"))\
                        .then_inc(v_stored[par], 16)

            def v_dst(c):
                return v_aug[bass.ds(c, 1), :, :, :].rearrange("a h p w -> p (a h) w")

            with sp.Fori(0, NG // 2 - 1) as it:
                store_parts(2 * it, it, False)
            store_parts(NG - 2, NG // 2 - 1, True)

            sp.wait_ge(guard_rows_ready, BATCH * SPLIT)
            for b in range(BATCH):
                with sp.Fori(0, CPB) as ci:
                    for o in range(QG):
                        sp.dma_start(guard[bass.ds(ci * HEADS + b * CPB * HEADS, HEADS), :, o * CH:o * CH + CH],
                                     guard_rows[0:P:DH, b, :, :]).then_inc(guard_stored, 16)
            sp.wait_ge(guard_stored, 16 * NG * QG)
            for o in range(QG + 1):
                sp.wait_ge(parts_stored[o], 16 * TERMS * (NG + 1))
            for par in range(2):
                sp.wait_ge(v_stored[par], 16 * (NG // 2 + 1))

            def load_qk(n, g, h, par, done):
                sp.dma_start(q_st[0:ROWS, par, :], q_aug[bass.ds(n, 1), :, :].rearrange("a r s -> (a r) s"))\
                    .then_inc(done, 16)
                b4 = (g // CPB) * CPB
                sp.dma_start(k_st[0:ROWS, par, :].rearrange("r (c s) -> r c s", c=CPB), k_src(b4, h)).then_inc(done, 16)

            def k_src(b4, h):
                return k_aug[bass.ds(b4 * HEADS, CPB * HEADS), :, :]\
                    .rearrange("(c h) r s -> h r c s", c=CPB)[h, :, :, :]

            sp.wait_ge(wide_ready, 1)
            bound_too_wide = sp.value_load(wide[0:1, 0:1], min_val=0, max_val=1)
            with sp.If(bound_too_wide):
                with sp.Fori(0, NG) as g:
                    for h in range(HEADS):
                        n = g * HEADS + h
                        sp.wait_ge(gm_stored, 16 * n + 16)
                        load_qk(n, g, h, 0, gm_loaded)
                        sp.wait_ge(gm_split, n + 1)
                        sp.dma_start(guard[bass.ds(n, 1), :, :].rearrange("a i (u p) -> u (a i) p", p=P),
                                     gm_parts[:, :, :]).then_inc(gm_stored, 16)
                sp.wait_ge(gm_stored, 16 * (NG * HEADS + 1))

            def load_block(g, h):
                n = g * HEADS + h
                par = h % 2
                if not (isinstance(g, int) and g == 0 and h < 2):
                    sp.wait_ge(pv_done, (n - 1) * UNITS)
                load_qk(n, g, h, par, operands_loaded[par])
                sp.dma_start(q_st[ROWS:AUG, par, :], guard[bass.ds(n, 1), :, :].rearrange("a i s -> (a i) s"))\
                    .then_inc(operands_loaded[par], 16)
                sp.dma_start(v_st[:, par, :, :].rearrange("p (c t) w -> p c (t w)", c=CPB), v_src((g // CPB) * CPB, h))\
                    .then_inc(operands_loaded[par], 16)

            def v_src(b4, h):
                return v_aug[bass.ds(b4, CPB), h, :, :].rearrange("c p w -> p c w")

            for h in range(HEADS):
                load_block(0, h)
            with sp.Fori(1, NG) as g:
                for h in range(HEADS // 2):
                    load_block(g, h)
                sp.wait_ge(y_ready, g * TPC + ONE_FREE)
                sp.dma_start(out_tiles[:, bass.ds((g - 1) * TPC, TPC), :], y_out[:, :, :]).then_inc(y_stored, 16)
                for h in range(HEADS // 2, HEADS):
                    load_block(g, h)
            sp.wait_ge(y_ready, NG * TPC + ONE_FREE)
            sp.dma_start(out_tiles[:, NT - TPC:NT, :], y_out[:, :, :]).then_inc(y_stored, 16)
            sp.wait_ge(y_stored, 16 * (NG + 1))

        @block.gpsimd
        def _(pool_e):
            pool_e.memset(ident[:, :], 0.0).then_inc(zeros_set, 1)
            pool_e.memset(ident_bf[:, :], 0.0).then_inc(zeros_set, 1)
            pool_e.memset(head_ones[:, :], 1.0).then_inc(zeros_set, 1)
            pool_e.wait_ge(zeros_set, 3)
            for m in (ident, ident_bf):
                pool_e.affine_select(out=m[:, :], in_=m[:, :], compare_op=ALU.not_equal, fill=1.0, base=0,
                                     pattern=[[-1, P]], channel_multiplier=1).then_inc(consts_set, 1)
            blocks = head_ones[:, :].rearrange("p (a b) -> p a b", b=DH)
            pool_e.affine_select(out=blocks, in_=blocks, compare_op=ALU.is_ge, fill=0.0, base=0,
                                 pattern=[[-DH, HEADS], [0, DH]], channel_multiplier=1).then_inc(zeros_set, 1)
            pool_e.wait_ge(zeros_set, 4)
            pool_e.affine_select(out=blocks, in_=blocks, compare_op=ALU.is_ge, fill=0.0, base=DH - 1,
                                 pattern=[[DH, HEADS], [0, DH]], channel_multiplier=-1).then_inc(consts_set, 1)
            pool_e.memset(minus_half[:, :], -0.5).then_inc(consts_set, 1)
            pool_e.memset(half[:, :], 0.5).then_inc(consts_set, 1)
            pool_e.memset(eps[:, :], LN_EPS).then_inc(consts_set, 1)
            pool_e.memset(v_tiles[:, :, :, :, DH:VW], 0.0).then_inc(zeros_set, 1)
            pool_e.wait_ge(zeros_set, 5)
            pool_e.memset(v_tiles[:, :, :, :, DH:DH + 1], 1.0).then_inc(ones_set, 1)
            pool_e.memset(ones_row[:, :], 1.0).then_inc(ones_set, 1)
            pool_e.wait_ge(ones_set, 2)
            pool_e.memset(k_st[ROWS:P, :, :], 1.0).then_inc(ones_set, 1)
            pool_e.wait_ge(consts_set, 6)
            pool_e.wait_ge(ones_set, 3)

            def rstd_of(c, par):
                pool_e.wait_ge(moments_ready, c + 1)
                pool_e.tensor_tensor(var_eps[:, :], moments[:, par, :, 1], eps[:, :], ALU.add)\
                    .then_inc(eps_added, 1)
                pool_e.wait_ge(eps_added, c + 1)
                pool_e.tensor_tensor(rstd[:, par, :], var_eps[:, :], minus_half[:, :], ALU.pow).then_inc(rstd_ready, 1)

            def chunk(c, par, last):
                for o in range(QG + 1):
                    if o == 2 and not last:
                        pool_e.wait_ge(sq_ready, c * (QG + 1) + o)
                        rstd_of(c + 1, 1 - par)
                        pool_e.wait_ge(rstd_ready, c + 2)
                    i = c * (QG + 1) + o
                    slot = (par * (QG + 1) + o) % 2
                    pool_e.wait_ge(part1_ready, i + 1)
                    pool_e.wait_ge(n2_ready, i)
                    pool_e.tensor_tensor(sq[:, slot, :], parts[:, o, 0, :], parts[:, o, 0, :], ALU.mult)\
                        .then_inc(sq_ready, 1)

            rstd_of(0, 0)
            pool_e.wait_ge(rstd_ready, 1)
            chunk(0, 0, False)
            chunk(1, 1, False)
            with pool_e.Fori(1, NG // 2 - 1) as it:
                chunk(2 * it, 0, False)
                chunk(2 * it + 1, 1, False)
            chunk(NG - 2, 0, False)
            chunk(NG - 1, 1, True)

            pool_e.wait_ge(sq_ready, NG * (QG + 1))
            pool_e.wait_ge(bound_in, 2)
            pool_e.tensor_tensor(bound[:, 4:6, :], bound[:, 2:4, :], half[:, :].rearrange("p (a b) -> p a b", a=2), ALU.pow)\
                .then_inc(bound_root, 1)
            pool_e.wait_ge(range_ready, 1)
            pool_e.partition_all_reduce(range_all[:, :], bound[:, 6, :], P, MAX_OVER_PARTITIONS).then_inc(bound_all, 1)
            pool_e.wait_ge(bound_all, 1)

            with pool_e.Fori(0, NG) as g:
                pool_e.wait_ge(f_moments, g + 1)
                pool_e.tensor_tensor(var_eps[:, :], moments[:, 0, :, 1], eps[:, :], ALU.add).then_inc(f_eps, 1)
                pool_e.wait_ge(f_eps, g + 1)
                pool_e.tensor_tensor(rstd[:, 0, :], var_eps[:, :], minus_half[:, :], ALU.pow).then_inc(f_rstd, 1)
                pool_e.wait_ge(f_rstd, g + 1)

        @block.scalar
        def _(act):
            act.dma_start(wq_raw[:, :, :], Wq.rearrange("(a p) i -> p a i", p=P)).then_inc(w_loaded, 16)
            act.dma_start(wkv_raw[:, 0, :], Wk).then_inc(w_loaded, 16)
            act.dma_start(wkv_raw[:, 1, :], Wv).then_inc(w_loaded, 16)
            act.dma_start(mem_w, memory_weight.partition_broadcast(P)).then_inc(small_loaded, 16)
            act.dma_start(ws_col, weight_scale.partition_broadcast(P)).then_inc(small_loaded, 16)
            act.dma_start(s_raw[:, :], input_scale.partition_broadcast(P)).then_inc(small_loaded, 16)
            act.dma_start(mem_aug[:, 0:KV], memory).then_inc(small_loaded, 16)
            act.dma_start(mem_aug[:, KV:KV + 1], memory_norm).then_inc(small_loaded, 16)
            act.sem_inc(xnT_ready, TWO_FREE)
            act.sem_inc(p32_ready, TWO_FREE)
            act.sem_inc(v_tile_ready, ONE_FREE)
            act.sem_inc(probs_ready, TWO_FREE)
            act.wait_ge(small_loaded, 80)
            act.activation(e_neg, mem_w, ACT.Exp, scale=-1.0).then_inc(e_neg_ready, 1)
            for j in range(3 * KT // 2):
                act.wait_ge(w_turned, j + 1)
                if j < KT:
                    dst, src = wqT[:, j, :], tp[j % 2]
                else:
                    dst = (wkT, wvT)[j - KT][:, :, :].rearrange("p k o -> p (k o)")
                    src = tp[j % 2]
                act.activation(dst, src, ACT.Copy).then_inc(w_copied, 1)

            def copy_xnT(c, par, first):
                if not first:
                    act.wait_ge(v_proj_ready, c)
                for k in range(KT):
                    act.wait_ge(tp_ready, c * KT + k + 1)
                    act.activation(xnT[:, par, k, :], tp[k % 2], ACT.Copy).then_inc(xnT_ready, 1)

            def exp_neg(c, par, o):
                act.wait_ge(neg_ready, c * QG + o + 1)
                act.wait_ge(sigma_ready, c * QG + o + 1)
                act.activation(epos[:, o % 2, :], neg[:, o % 2, :], ACT.Exp).then_inc(epos_ready, 1)

            def second_part(c, par, o):
                act.wait_ge(rest_ready, c * (QG + 1) + o + 1 + TWO_FREE)
                act.activation(parts[:, o, 1, :], r32[:, (par * (QG + 1) + o) % 2, :], ACT.Copy).then_inc(part2_ready, 1)

            def chunk(c, par, last):
                for o in range(QG + 1):
                    i = c * (QG + 1) + o
                    slot = (par * (QG + 1) + o) % 2
                    act.wait_ge(proj_ready, i + 1)
                    act.wait_ge(rest_ready, i + 1)
                    act.activation(p32[:, slot, :], pj[slot], ACT.Copy).then_inc(p32_ready, 1)
                    if o >= 1:
                        exp_neg(c, par, o - 1)
                        second_part(c, par, o - 1)
                second_part(c, par, QG)
                act.wait_ge(v_proj_ready, c + 1 + ONE_FREE)
                act.wait_ge(v_stored[par], (c - par) * 8 + 16)
                act.wait_ge(scal, 4)
                act.activation(v_tiles[:, par, :, :, 0:DH], vp.rearrange("p (t h d) -> p h t d", t=TPC, h=HEADS),
                               ACT.Copy, scale=w_dot).then_inc(v_tile_ready, 1)
                if not last:
                    copy_xnT(c + 1, 1 - par, False)

            copy_xnT(0, 0, True)
            with act.Fori(0, NG // 2 - 1) as it:
                chunk(2 * it, 0, False)
                chunk(2 * it + 1, 1, False)
            chunk(NG - 2, 0, False)
            chunk(NG - 1, 1, True)
            with act.Fori(0, NG * HEADS // 2) as pair:
                for v in range(2 * UNITS):
                    act.wait_ge(scores_ready, pair * (2 * UNITS) + v + 1)
                    width = len(strips(v % UNITS)) * CH
                    act.activation(probs[:, v % PSLOTS, 0:width],
                                   sc[v % SLOTS][:, :, :].rearrange("p a b -> p (a b)")[:, 0:width], ACT.Exp,
                                   scale=SCALE).then_inc(probs_ready, 1)

        @block.tensor
        def _(pe):
            pe.sem_inc(v_proj_ready, ONE_FREE)
            pe.sem_inc(am_ready, ONE_FREE)
            pe.wait_ge(consts_set, 6)
            pe.wait_ge(w_loaded, 48)
            for j in range(KT + 2):
                if j >= 2:
                    pe.wait_ge(w_copied, j - 1)
                for a in range(KT):
                    src = wq_raw[:, a, j * P:j * P + P] if j < KT else wkv_raw[:, j - KT, a * P:a * P + P]
                    last = pe.transpose(tp[j % 2][:, a * P:a * P + P], src, ident[:, :])
                last.then_inc(w_turned, 1)
            pe.wait_ge(w_copied, KT + 2)

            def turn_xn(c):
                pe.wait_ge(xn_ready, c + 1)
                for k in range(KT):
                    pe.wait_ge(xnT_ready, c * KT + k + 1)
                    for t in range(TPC):
                        last = pe.transpose(tp[k % 2][:, t * P:t * P + P], xn[:, t, k * P:k * P + P], ident[:, :])
                    last.then_inc(tp_ready, 1)

            def norms(c, par, o):
                i = c * (QG + 1) + o
                pe.wait_ge(sq_ready, i + 1)
                pe.wait_ge(n2_used, i + 1)
                pe.matmul(n2, head_ones[:, :], sq[:, (par * (QG + 1) + o) % 2, :], start=True, stop=True)\
                    .then_inc(n2_ready, 1)

            def chunk(c, par, last_chunk):
                pe.wait_ge(xnT_ready, (c + 1) * KT + TWO_FREE)
                for o in range(QG + 1):
                    i = c * (QG + 1) + o
                    pe.wait_ge(p32_ready, i + 1)
                    for k in range(KT):
                        w = wqT[:, k, o * P:o * P + P] if o < QG else wkT[:, k, :]
                        last = pe.matmul(pj[(par * (QG + 1) + o) % 2], w, xnT[:, par, k, :],
                                         start=(k == 0), stop=(k == KT - 1))
                    last.then_inc(proj_ready, 1)
                    if o >= 1:
                        norms(c, par, o - 1)
                pe.wait_ge(v_tile_ready, c + 1)
                for t in range(TPC):
                    for k in range(KT):
                        last = pe.matmul(vp[:, t * P:t * P + P], xnT[:, par, k, t * P:t * P + P], wvT[:, k, :],
                                         start=(k == 0), stop=(k == KT - 1))
                last.then_inc(v_proj_ready, 1)
                norms(c, par, QG)
                if not last_chunk:
                    turn_xn(c + 1)
                pe.wait_ge(sigma_ready, (c + 1) * QG + TWO_FREE)
                pe.wait_ge(scal, 4)
                for t in range(TPC):
                    for hf in range(2):
                        pe.wait_ge(am_used, c * (2 * TPC) + 2 * t + hf + 1)
                        for q in range(2):
                            last = pe.matmul(am[hf][:, q, :], sigma[:, 2 * hf + q, t * P:t * P + P], mem_aug[:, :],
                                             start=True, stop=True)
                        last.then_inc(am_ready, 1)

            turn_xn(0)
            with pe.Fori(0, NG // 2 - 1) as it:
                chunk(2 * it, 0, False)
                chunk(2 * it + 1, 1, False)
            chunk(NG - 2, 0, False)
            chunk(NG - 1, 1, True)

            pe.wait_ge(k_mean_ready, 1)
            pe.matmul(n2[:, 0:BATCH], head_ones[:, :], k_mean_sq[:, :], start=True, stop=True).then_inc(k_mean_norm, 1)

            pe.wait_ge(wide_ready, 1)
            bound_too_wide = pe.value_load(wide[0:1, 0:1], min_val=0, max_val=1)
            with pe.If(bound_too_wide):
                with pe.Fori(0, NG * HEADS) as n:
                    pe.wait_ge(gm_loaded, n * 32 + 32)
                    for u in range(QG * TPC):
                        pe.wait_ge(gm_scores_used, n * (QG * TPC) + u + ONE_FREE)
                        for c4 in range(CPB):
                            last = pe.matmul(ps[:, c4, :], q_st[0:ROWS, 0, u * P:u * P + P],
                                             k_st[0:ROWS, 0, c4 * CH:c4 * CH + CH], start=True, stop=True)
                        last.then_inc(gm_scores, 1)
                    pe.wait_ge(gm_scores_used, n * (QG * TPC) + QG * TPC + ONE_FREE)
                    pe.transpose(ps[0:QG * TPC, 6, 0:P], row_max[:, :], ident[:, :]).then_inc(gm_turned, 1)

            def scores(n, par, u):
                pe.wait_ge(probs_ready, n * UNITS + u + 1)
                for i in strips(u):
                    j, q = divmod(i, QG)
                    last = pe.matmul(sc[u % SLOTS][:, i % UNIT, :], k_st[0:AUG, par, j * P:j * P + P],
                                     q_st[0:AUG, par, q * CH:q * CH + CH], start=True, stop=True)
                last.then_inc(scores_ready, 1)

            def weigh_v(n, par, u):
                for i in strips(u):
                    j, q = divmod(i, QG)
                    last = pe.matmul(acc[par][VW * q:VW * q + VW, :], v_st[:, par, j, :],
                                     probs[:, (par * UNITS + u) % PSLOTS, (i % UNIT) * CH:(i % UNIT) * CH + CH],
                                     start=(j == 0), stop=(j == ST - 1))
                last.then_inc(pv_done, 1)

            def turn_out(n, par):
                pe.wait_ge(oT_ready, n + 1)
                for t in range(TPC):
                    last = pe.transpose(acc[par][:, t * P:t * P + P], oT[:, par, t * P:t * P + P], ident[:, :])
                last.then_inc(tr_ready, 1)

            def ffn_turn(g, t):
                if t == 0:
                    pe.wait_ge(xq_ready, g + 1)
                pe.wait_ge(y_ready, g * TPC + t + ONE_FREE)
                for k in range(KT):
                    last = pe.transpose(ffn_tp[:, k * P:k * P + P], xq[:, t, k * P:k * P + P], ident_bf[:, :])
                last.then_inc(xq_turned, 1)

            def ffn_product(g, t):
                pe.wait_ge(xqT_ready, g * TPC + t + 1)
                for k in range(KT):
                    last = pe.matmul(ffn_ps, xqT[:, k, :], wT_ffn[:, k, :], start=(k == 0), stop=(k == KT - 1))
                last.then_inc(ffn_ready, 1)

            def turn_ffn_weight(k):
                pe.wait_ge(dec, 8)
                pe.wait_ge(wf_copied, k)
                for a in range(KT):
                    last = pe.transpose(ffn_wtp[:, a * P:a * P + P], w_val[:, a, k * P:k * P + P], ident_bf[:, :])
                last.then_inc(wf_turned, 1)

            def pair(n0, trip, first=False, ffn_g=None, ffn_read=None):
                for par in range(2):
                    n = n0 + par
                    pe.wait_ge(operands_loaded[par], trip * 64 + 64)
                    for u in range(UNITS):
                        scores(n, par, u)
                        if u >= SLOTS:
                            if u == SLOTS:
                                pe.wait_ge(head_out_ready, n + 1)
                                if first and par == 1:
                                    pe.wait_ge(wf_copied, KT)
                                if ffn_read is not None and par == 0:
                                    pe.wait_ge(y_ready, ffn_read)
                            weigh_v(n, par, u - SLOTS)
                        elif not (first and par == 0):
                            weigh_v(n - 1, 1 - par, UNITS + u - SLOTS)
                        if first and par == 0:
                            if u >= 8 and u % 2 == 0 and u < 8 + 2 * KT:
                                turn_ffn_weight((u - 8) // 2)
                        elif u == TURN_AT:
                            turn_out(n - 1, 1 - par)
                        if ffn_g is not None and par == 1 and u in FFN_AT:
                            step = FFN_AT.index(u)
                            if step == 0:
                                pe.wait_ge(head_out_ready, n + TWO_FREE)
                            (ffn_turn, ffn_product)[step % 2](ffn_g, step // 2)

            pairs = HEADS // 2
            pair(0, 0, first=True)
            with pe.Fori(1, pairs) as hp:
                pair(2 * hp, hp)
            with pe.Fori(1, NG) as g:
                pair(g * HEADS, g * pairs, ffn_g=g - 1)
                with pe.Fori(1, pairs) as hp:
                    pair(g * HEADS + 2 * hp, g * pairs + hp, ffn_read=g * TPC + ONE_FREE)
            last_n = NG * HEADS - 1
            for u in range(UNITS - SLOTS, UNITS):
                pe.wait_ge(probs_ready, last_n * UNITS + u + 1 + TWO_FREE)
                weigh_v(last_n, 1, u)
            turn_out(last_n, 1)
            for t in range(TPC):
                ffn_turn(NG - 1, t)
                ffn_product(NG - 1, t)

        @block.vector
        def _(dve):
            dve.sem_inc(rest_ready, TWO_FREE)
            dve.sem_inc(sigma_ready, TWO_FREE)
            dve.sem_inc(am_used, TWO_FREE)
            dve.sem_inc(head_out_ready, TWO_FREE)
            dve.sem_inc(n2_used, ONE_FREE)
            dve.sem_inc(gm_scores_used, ONE_FREE)
            dve.sem_inc(y_ready, ONE_FREE)

            def statistics(c):
                for t in range(TPC):
                    last = dve.bn_stats(stats[:, t, :], resid[:, bass.ds(c * TPC + t, 1), :].rearrange("p a d -> p (a d)"))
                last.then_inc(stats_ready, 1)

            def mean_and_variance(par):
                for t in range(TPC):
                    last = dve.bn_aggr(moments[:, par, t, :], stats[:, t, :])
                last.then_inc(moments_ready, 1)

            def normalise(c, par):
                dve.wait_ge(rstd_ready, c + 1)
                dve.wait_ge(tp_ready, c * KT)
                for t in range(TPC):
                    last = dve.tensor_scalar(xn[:, t, :], resid[:, bass.ds(c * TPC + t, 1), :].rearrange("p a d -> p (a d)"),
                                             moments[:, par, t, 0:1], rstd[:, par, t:t + 1], ALU.subtract, ALU.mult)
                last.then_inc(xn_ready, 1)

            dve.wait_ge(x_loaded[0], 16)
            statistics(0)
            dve.wait_ge(stats_ready, 1)
            mean_and_variance(0)
            dve.wait_ge(e_neg_ready, 1)
            dve.tensor_scalar(one_plus, e_neg, 1.0, None, ALU.add).then_inc(scal, 1)
            dve.wait_ge(scal, 1)
            dve.reciprocal(w_mem, one_plus).then_inc(scal, 1)
            dve.wait_ge(scal, 2)
            dve.tensor_scalar(w_dot, w_mem, -1.0, 1.0, ALU.mult, ALU.add).then_inc(scal, 1)
            dve.tensor_scalar(mem_aug[:, 0:KV], mem_aug[:, 0:KV], w_mem, None, ALU.mult).then_inc(scal, 1)
            dve.tensor_copy(s_col, s_raw[:, :]).then_inc(scal, 1)
            dve.wait_ge(scal, 5)
            dve.reciprocal(inv_s, s_col).then_inc(scal, 1)
            dve.tensor_tensor(sw, s_col, ws_col, ALU.mult).then_inc(scal, 1)
            normalise(0, 0)

            def finish(c, par, o):
                i = c * (QG + 1) + o
                slot = (par * (QG + 1) + o) % 2
                dve.wait_ge(part2_ready, i + 1)
                dve.tensor_tensor(parts[:, o, 2, :], r32[:, slot, :], parts[:, o, 1, :], ALU.subtract)\
                    .then_inc(part3_ready, 1)
                if o < QG:
                    dve.wait_ge(epos_ready, c * QG + o + 1)
                    dve.wait_ge(am_ready, c * (2 * TPC) + ONE_FREE)
                    dve.scalar_tensor_tensor(sigma[:, o, :], epos[:, o % 2, :], -1.0, relu[:, o % 2, :],
                                             ALU.add, ALU.add).then_inc(sigma_ready, 1)
                dve.wait_ge(n2_ready, i + 1)
                dve.tensor_reduce(norm2[:, bass.ds(c, 1), o], n2, AX.X, ALU.max).then_inc(n2_used, 1)

            def chunk(c, par, last_chunk):
                for o in range(QG + 1):
                    i = c * (QG + 1) + o
                    slot = (par * (QG + 1) + o) % 2
                    if o == 1 and not last_chunk:
                        dve.wait_ge(stats_ready, c + 2)
                    dve.wait_ge(p32_ready, i + 1 + TWO_FREE)
                    dve.wait_ge(parts_stored[o], (c + 1) * (16 * TERMS))
                    dve.tensor_copy(parts[:, o, 0, :], p32[:, slot, :]).then_inc(part1_ready, 1)
                    if o == 1 and not last_chunk:
                        mean_and_variance(1 - par)
                    if o < QG:
                        dve.tensor_scalar(neg[:, o % 2, :], p32[:, slot, :], 0.0, None, ALU.min).then_inc(neg_ready, 1)
                        dve.wait_ge(sigma_ready, c * QG + o + 1)
                        dve.tensor_scalar(relu[:, o % 2, :], p32[:, slot, :], 0.0, None, ALU.max).then_inc(relu_ready, 1)
                    else:
                        dve.tensor_reduce(k_sum[:, bass.ds(c, 1)], p32[:, slot, :], AX.X, ALU.add)
                    if o == 0 and not last_chunk:
                        dve.wait_ge(x_loaded[1 - par], (c + par) * 8 + 16)
                    dve.wait_ge(part1_ready, i + 1)
                    dve.tensor_tensor(r32[:, slot, :], p32[:, slot, :], parts[:, o, 0, :], ALU.subtract)\
                        .then_inc(rest_ready, 1)
                    if o == 0 and not last_chunk:
                        statistics(c + 1)
                    if o == 2 and not last_chunk:
                        normalise(c + 1, 1 - par)
                    if o >= 1:
                        finish(c, par, o - 1)
                finish(c, par, QG)
                for t in range(TPC):
                    for hf in range(2):
                        k = c * (2 * TPC) + 2 * t + hf
                        dve.wait_ge(am_ready, k + 1 + ONE_FREE)
                        dve.reciprocal(rnorm[:, hf, :], am[hf][:, :, KV]).then_inc(rnorm_ready, 1)
                        dve.wait_ge(rnorm_ready, k + 1)
                        for q in range(2):
                            o = 2 * hf + q
                            row = resid[:, bass.ds(c * TPC + t, 1), o * KV:o * KV + KV].rearrange("p a d -> p (a d)")
                            last = dve.scalar_tensor_tensor(row, am[hf][:, q, 0:KV], rnorm[:, hf, q:q + 1], row,
                                                            ALU.mult, ALU.add)
                        last.then_inc(am_used, 1)

            with dve.Fori(0, NG // 2 - 1) as it:
                chunk(2 * it, 0, False)
                chunk(2 * it + 1, 1, False)
            chunk(NG - 2, 0, False)
            chunk(NG - 1, 1, True)

            dve.wait_ge(n2_used, NG * (QG + 1) + ONE_FREE)
            by_batch = norm2[:, :, :].rearrange("p (b c) o -> p b c o", b=BATCH)
            dve.tensor_reduce(k_total[:, :], k_sum[:, :].rearrange("p (b c) -> p b c", b=BATCH), AX.X, ALU.add).then_inc(gd, 1)
            dve.tensor_reduce(bound[:, 0, :], by_batch[:, :, :, 0:QG], AX.XY, ALU.max).then_inc(gd, 1)
            dve.tensor_reduce(bound[:, 1, :], by_batch[:, :, :, QG], AX.X, ALU.max).then_inc(gd, 1)
            dve.wait_ge(gd, 1)
            dve.scalar_tensor_tensor(k_mean_sq[:, :], k_total[:, :], 1.0 / SEQ ** 2, k_total[:, :], ALU.mult, ALU.mult)\
                .then_inc(k_mean_ready, 1)
            dve.wait_ge(gd, 3)
            dve.tensor_tensor(bound[:, 2, :], bound[:, 0, :], bound[:, 1, :], ALU.mult).then_inc(bound_in, 1)
            dve.wait_ge(k_mean_norm, 1)
            dve.tensor_tensor(bound[:, 3, :], bound[:, 0, :], n2[:, 0:BATCH], ALU.mult).then_inc(bound_in, 1)
            dve.wait_ge(bound_root, 1)
            dve.tensor_tensor(bound[:, 6, :], bound[:, 4, :], bound[:, 5, :], ALU.add).then_inc(range_ready, 1)
            dve.tensor_tensor(bound[:, 7, :], bound[:, 4, :], bound[:, 5, :], ALU.subtract).then_inc(gd, 1)
            dve.wait_ge(gd, 4)
            dve.tensor_scalar(bound[:, 8, :], bound[:, 7, :], -GUARD_MARGIN / 2, GUARD_OFFSET, ALU.mult, ALU.add).then_inc(gd, 1)
            dve.wait_ge(gd, 5)
            dve.tensor_copy(guard_bf[:, :, 0], bound[:, 8, :]).then_inc(gd, 1)
            dve.wait_ge(gd, 6)
            dve.tensor_tensor(guard_rest[:, :], bound[:, 8, :], guard_bf[:, :, 0], ALU.subtract).then_inc(gd, 1)
            dve.wait_ge(gd, 7)
            dve.tensor_copy(guard_bf[:, :, 1], guard_rest[:, :]).then_inc(gd, 1)
            dve.wait_ge(gd, 8)
            dve.tensor_tensor(guard_bf[:, :, 2], guard_rest[:, :], guard_bf[:, :, 1], ALU.subtract).then_inc(gd, 1)
            dve.wait_ge(gd, 9)
            dve.tensor_copy(guard_parts[:, :, :], guard_bf[:, :, :]).then_inc(gd, 1)
            dve.wait_ge(gd, 10)
            dve.wait_ge(ones_set, 3)
            for b in range(BATCH):
                for i in range(SPLIT):
                    dve.tensor_scalar(guard_rows[:, b, i, :], ones_row[:, :], guard_parts[:, b, i:i + 1], None, ALU.mult)\
                        .then_inc(guard_rows_ready, 1)
            dve.wait_ge(bound_all, 1)
            dve.tensor_reduce(widest[:, :], range_all[:, :], AX.X, ALU.max).then_inc(gd, 1)
            dve.wait_ge(gd, 11)
            dve.tensor_scalar(wide[:, :], widest[:, :], GUARD_LIMIT, None, ALU.is_gt).then_inc(wide_ready, 1)
            dve.wait_ge(wide_ready, 1)
            bound_too_wide = dve.value_load(wide[0:1, 0:1], min_val=0, max_val=1)
            with dve.If(bound_too_wide):
                with dve.Fori(0, NG * HEADS) as n:
                    for u in range(QG * TPC):
                        dve.wait_ge(gm_scores, n * (QG * TPC) + u + 1)
                        dve.tensor_reduce(row_max[:, u:u + 1], ps[:, 0:CPB, :], AX.XY, ALU.max).then_inc(gm_scores_used, 1)
                    dve.wait_ge(gm_turned, n + 1)
                    turned = ps[0:QG * TPC, 6, 0:P]
                    dve.tensor_scalar(gm_parts[:, 0, :], turned, -1.0, None, ALU.mult).then_inc(gm_step, 1)
                    dve.wait_ge(gm_step, n * 3 + 1)
                    dve.scalar_tensor_tensor(gm_rest[:, :], turned, -1.0, gm_parts[:, 0, :], ALU.mult, ALU.subtract)\
                        .then_inc(gm_step, 1)
                    dve.wait_ge(gm_step, n * 3 + 2)
                    dve.tensor_copy(gm_parts[:, 1, :], gm_rest[:, :]).then_inc(gm_step, 1)
                    dve.wait_ge(gm_step, n * 3 + 3)
                    dve.tensor_tensor(gm_parts[:, 2, :], gm_rest[:, :], gm_parts[:, 1, :], ALU.subtract).then_inc(gm_split, 1)

            dve.wait_ge(w8_loaded, 16)
            mag, sign, twice = work[:, 0:4, :], work[:, 4:8, :], y_out[:, :, :]
            dve.tensor_copy(mag, w8[:, :, :].bitcast(U8)).then_inc(dec, 1)
            dve.wait_ge(dec, 1)
            dve.tensor_scalar(sign, mag, 128.0, 128.0, ALU.is_ge, ALU.mult).then_inc(dec, 1)
            dve.wait_ge(dec, 2)
            dve.tensor_tensor(mag, mag, sign, ALU.subtract).then_inc(dec, 1)
            dve.wait_ge(dec, 3)
            dve.tensor_scalar(mag.bitcast(I32), mag, 960.0, 2.0 ** 20, ALU.add, ALU.mult).then_inc(dec, 1)
            dve.wait_ge(dec, 4)
            dve.tensor_scalar(twice, mag, 2.0, -2.0 ** -6, ALU.mult, ALU.add).then_inc(dec, 1)
            dve.wait_ge(dec, 5)
            dve.tensor_tensor(mag, mag, twice, ALU.min).then_inc(dec, 1)
            dve.tensor_scalar(sign, sign, -2.0 / 128.0, 1.0, ALU.mult, ALU.add).then_inc(dec, 1)
            dve.wait_ge(dec, 7)
            dve.tensor_tensor(w_val[:, :, :], mag, sign, ALU.mult).then_inc(dec, 1)
            for k in range(KT):
                dve.wait_ge(wf_turned, k + 1)
                dve.tensor_copy(wT_ffn[:, k, :], ffn_wtp).then_inc(wf_copied, 1)

            def add_head(n, par, g, h):
                dve.wait_ge(pv_done, n * UNITS + UNITS)
                dve.tensor_copy(oT[:, par, :], acc[par]).then_inc(oT_ready, 1)
                dve.wait_ge(tr_ready, n + 1)
                dve.reciprocal(rden[:, :, :], tr[par][:, :, :, DH]).then_inc(rden_ready, 1)
                dve.wait_ge(rden_ready, n + 1)
                dve.tensor_tensor(head_out[:, :, :, :], tr[par][:, :, :, 0:DH],
                                  rden[:, :, :].unsqueeze(3).to_broadcast([P, TPC, QG, DH]), ALU.mult)\
                    .then_inc(head_out_ready, 1)
                dve.wait_ge(head_out_ready, n + 1 + TWO_FREE)
                cols = resid[:, bass.ds(g * TPC, TPC), :].rearrange("p t (q f) -> p t q f", q=QG)[:, :, :, bass.ds(h * DH, DH)]
                dve.tensor_tensor(cols, cols, head_out[:, :, :, :], ALU.add)

            def round_to_float8(g):
                dve.drain()
                for t in range(TPC):
                    dve.bn_stats(stats[:, t, :], resid[:, bass.ds(g * TPC + t, 1), :].rearrange("p a d -> p (a d)"))
                dve.drain()
                for t in range(TPC):
                    last = dve.bn_aggr(moments[:, 0, t, :], stats[:, t, :])
                last.then_inc(f_moments, 1)
                dve.wait_ge(f_rstd, g + 1)
                dve.tensor_scalar(rstd_s[:, :], rstd[:, 0, :], inv_s, None, ALU.mult).then_inc(f_step, 1)
                dve.wait_ge(f_step, g * 6 + 1)
                xs, big = work[:, 0:4, :], work[:, 4:8, :]
                for t in range(TPC):
                    last = dve.tensor_scalar(work[:, t, :], resid[:, bass.ds(g * TPC + t, 1), :].rearrange("p a d -> p (a d)"),
                                             moments[:, 0, t, 0:1], rstd_s[:, t:t + 1], ALU.subtract, ALU.mult)
                last.then_inc(f_step, 1)
                dve.wait_ge(f_step, g * 6 + 2)
                dve.tensor_scalar(xs, xs, FP8_MAX, -FP8_MAX, ALU.min, ALU.max).then_inc(f_step, 1)
                dve.wait_ge(f_step, g * 6 + 3)
                dve.tensor_scalar(big.bitcast(I32), xs.bitcast(I32), 0x7F800000, None, ALU.bitwise_and).then_inc(f_step, 1)
                dve.wait_ge(f_step, g * 6 + 4)
                dve.tensor_scalar(big, big, 2.0 ** -6, 1.5 * 2.0 ** 20, ALU.max, ALU.mult).then_inc(f_step, 1)
                dve.wait_ge(f_step, g * 6 + 5)
                dve.tensor_tensor(xs, xs, big, ALU.add).then_inc(f_step, 1)
                dve.wait_ge(f_step, g * 6 + 6)
                dve.tensor_tensor(xq, xs, big, ALU.subtract).then_inc(xq_ready, 1)

            def ffn_out(g):
                for t in range(TPC):
                    dve.wait_ge(xq_turned, g * TPC + t + 1)
                    dve.tensor_copy(xqT[:, :, :].rearrange("p k s -> p (k s)"), ffn_tp).then_inc(xqT_ready, 1)
                    dve.wait_ge(ffn_ready, g * TPC + t + 1)
                    if t == 0:
                        dve.wait_ge(y_stored, g * 16 + 16)
                    dve.scalar_tensor_tensor(y_out[:, t, :], ffn_ps, sw,
                                             resid[:, bass.ds(g * TPC + t, 1), :].rearrange("p a d -> p (a d)"),
                                             ALU.mult, ALU.add).then_inc(y_ready, 1)

            with dve.Fori(0, HEADS // 2) as hp:
                for par in range(2):
                    add_head(2 * hp + par, par, 0, 2 * hp + par)
            round_to_float8(0)
            with dve.Fori(1, NG) as g:
                add_head(g * HEADS, 0, g, 0)
                ffn_out(g - 1)
                add_head(g * HEADS + 1, 1, g, 1)
                with dve.Fori(1, HEADS // 2) as hp:
                    for par in range(2):
                        add_head(g * HEADS + 2 * hp + par, par, g, 2 * hp + par)
                round_to_float8(g)
            ffn_out(NG - 1)


def kernel(L0_attn_x, L0_attn_Wq, L0_attn_Wk, L0_attn_Wv, L0_attn_memory, L0_attn_memory_norm, L0_attn_memory_weight,
           L0_ffn_weight, L0_ffn_weight_scale, L0_ffn_input_scale):
    import concourse.bacc as bacc
    from concourse.bass_utils import run_bass_kernel_spmd

    nc = bacc.Bacc("TRN2", target_bir_lowering=False, num_devices=1)
    inputs = {
        "x": np.ascontiguousarray(L0_attn_x).reshape(BATCH * SEQ, DM),
        "Wq": np.ascontiguousarray(L0_attn_Wq),
        "Wk": np.ascontiguousarray(L0_attn_Wk),
        "Wv": np.ascontiguousarray(L0_attn_Wv),
        "memory": np.ascontiguousarray(L0_attn_memory),
        "memory_norm": np.ascontiguousarray(L0_attn_memory_norm),
        "memory_weight": np.ascontiguousarray(L0_attn_memory_weight),
        "weight": np.ascontiguousarray(L0_ffn_weight),
        "weight_scale": np.ascontiguousarray(L0_ffn_weight_scale).reshape(1),
        "input_scale": np.ascontiguousarray(L0_ffn_input_scale).reshape(1),
    }
    aps = [nc.dram_tensor(f"in_{name}", a.shape, mybir.dt.from_np(a.dtype), kind="ExternalInput").ap()
           for name, a in inputs.items()]
    out = nc.dram_tensor("out", (BATCH * SEQ, DM), F32, kind="ExternalOutput").ap()
    q_aug = nc.dram_tensor("q_aug", (NG * HEADS, ROWS, QG * CH), BF16, kind="Internal").ap()
    k_aug = nc.dram_tensor("k_aug", (NG * HEADS, ROWS, CH), BF16, kind="Internal").ap()
    v_aug = nc.dram_tensor("v_aug", (NG, HEADS, P, TPC * VW), F32, kind="Internal").ap()
    guard = nc.dram_tensor("guard", (NG * HEADS, SPLIT, QG * CH), BF16, kind="Internal").ap()
    attention_ffn(nc, *aps, out, q_aug, k_aug, v_aug, guard)
    r = run_bass_kernel_spmd(nc, [{f"in_{name}": a for name, a in inputs.items()}], core_ids=[0])
    return r.results[0]["out"].reshape(BATCH, SEQ, DM)
```

```python
from contextlib import ExitStack

import concourse.bass as bass
import numpy as np
from concourse import mybir
from concourse.alu_op_type import AluOpType as ALU

F32 = mybir.dt.float32
BF16 = mybir.dt.bfloat16
I32 = mybir.dt.int32
U8 = mybir.dt.uint8
ACT = mybir.ActivationFunctionType
AX = mybir.AxisListType
MAX_OVER_PARTITIONS = bass.bass_isa.ReduceOp.max

P = 128
BATCH, SEQ, DM = 2, 2048, 512
HEADS, QG, DH = 8, 4, 16
KV = HEADS * DH
CH = 512
CPB = SEQ // CH
NG = BATCH * CPB
TPC = CH // P
KT = DM // P
NT = NG * TPC
ST = SEQ // P
VW = 32
SPLIT = 3
Q_PART = (0, 0, 0, 1, 1, 2)
K_PART = (0, 1, 2, 0, 1, 0)
TERMS = len(Q_PART)
ROWS = TERMS * DH
AUG = ROWS + SPLIT
SCALE = DH ** -0.5
LN_EPS = 1e-5
FP8_MAX = 448.0
ONE_FREE, TWO_FREE, THREE_FREE = 1, 2, 3
STRIPS = QG * ST
UNIT = 2
UNITS = STRIPS // UNIT
UNITS_OF_TILE = QG // UNIT
SLOTS = 3
PSLOTS = 8
GUARD_MARGIN = 1.02
GUARD_LIMIT = 130.0 / (SCALE * GUARD_MARGIN)
GUARD_OFFSET = 3.0 / SCALE
TURN_AT = 6
W_TURN_AT = UNITS - 3 * KT
FFN_AT = tuple(range(11, 11 + 4 * TPC, 2))


def units_since(u):
    return SLOTS if u >= SLOTS else u + UNITS - max(w for w in range(UNITS) if w % SLOTS == u)


def attention_ffn(nc, x, Wq, Wk, Wv, memory, memory_norm, memory_weight, weight, weight_scale, input_scale, out,
                  q_aug, k_aug, v_aug, guard):
    x_tiles = x.rearrange("(t p) d -> p t d", p=P)
    out_tiles = out.rearrange("(t p) d -> p t d", p=P)

    with ExitStack() as ctx:
        def sb(name, shape, dt):
            return ctx.enter_context(nc.sbuf_tensor(name, shape, dt))

        def sem(name):
            return ctx.enter_context(nc.semaphore(name))

        ps = ctx.enter_context(nc.psum_tensor("ps", [P, 8, 512], F32))

        resid = sb("resid", [P, NT, DM], F32)
        ident = sb("ident", [P, P], F32)
        ident_bf = sb("ident_bf", [P, P], BF16)
        head_ones = sb("head_ones", [P, P], BF16)
        minus_half = sb("minus_half", [P, TPC], F32)
        eps = sb("eps", [P, TPC], F32)
        half = sb("half", [P, 2 * BATCH], F32)
        k_sum = sb("k_sum", [P, NG], F32)
        k_total = sb("k_total", [P, BATCH], F32)
        k_mean_sq = sb("k_mean_sq", [P, BATCH], BF16)
        wT_ffn = sb("wT_ffn", [P, KT, DM], BF16)
        scalars = sb("scalars", [P, 10], F32)
        mem_w, e_neg, one_plus, w_mem, w_dot, ws_col, s_col, inv_s, sw = (scalars[:, i:i + 1] for i in range(9))
        s_raw = sb("s_raw", [P, 1], BF16)
        q_st = sb("q_st", [P, 2, QG * CH], BF16)
        k_st = sb("k_st", [P, 2, SEQ], BF16)
        v_st = sb("v_st", [P, 2, ST, VW], F32)
        pool = sb("pool", [P, 8192], F32)
        probs = pool[:, 0:PSLOTS * UNIT * CH].rearrange("p (a b) -> p a b", a=PSLOTS)
        oT = sb("oT", [P, 2, CH], F32)
        rden = sb("rden", [P, TPC, QG], F32)
        head_out = sb("head_out", [P, TPC, QG, DH], F32)
        xnT = pool[:, 0:4096].rearrange("p (a k s) -> p a k s", a=2, k=KT)
        xn = pool[:, 4096:6144].rearrange("p (t d) -> p t d", t=TPC)
        sigma = pool[:, 6144:8192].rearrange("p (o s) -> p o s", o=QG)
        wqT = sb("wqT", [P, KT, DM], F32)
        wkT = sb("wkT", [P, KT, KV], F32)
        wvT = sb("wvT", [P, KT, KV], F32)
        mem_aug = sb("mem_aug", [P, KV + 1], F32)
        parts = sb("parts", [P, QG + 1, SPLIT, CH], BF16)
        sq = sb("sq", [P, 2, CH], BF16)
        v_tiles = sb("v_tiles", [P, 2, HEADS, TPC, VW], F32)
        work = sb("work", [P, 10, CH], F32)
        p32, r32, neg, epos, relu = (work[:, 2 * i:2 * i + 2, :] for i in range(5))
        y_out = sb("y_out", [P, TPC, DM], F32)
        wq_raw = y_out
        wkv_raw = sb("wkv_raw", [P, 2, DM], F32)
        xq = wkv_raw[:, :, :].bitcast(BF16).rearrange("p a (b d) -> p (a b) d", b=2)
        w8 = sb("w8", [P, KT, DM], mybir.dt.float8e4)
        w_val = sb("w_val", [P, KT, DM], BF16)
        xqT = sb("xqT", [P, KT, P], BF16)
        stats = sb("stats", [P, TPC, 6], F32)
        moments = sb("moments", [P, 2, TPC, 2], F32)
        var_eps = sb("var_eps", [P, TPC], F32)
        rstd = sb("rstd", [P, 2, TPC], F32)
        rstd_s = sb("rstd_s", [P, TPC], F32)
        rnorm = sb("rnorm", [P, 2, 2], F32)
        norm2 = sb("norm2", [P, NG, QG + 1], F32)
        bound = sb("bound", [P, 9, BATCH], F32)
        range_all = sb("range_all", [P, BATCH], F32)
        widest = sb("widest", [P, 1], F32)
        guard_rest = sb("guard_rest", [P, BATCH], F32)
        guard_parts = sb("guard_parts", [P, BATCH, SPLIT], F32)
        guard_bf = sb("guard_bf", [P, BATCH, SPLIT], BF16)
        ones_row = sb("ones_row", [P, CH], BF16)
        guard_rows = pool[:, 0:BATCH * SPLIT * QG * CH // 2].bitcast(BF16)\
            .rearrange("p (b i o s) -> p b i o s", b=BATCH, i=SPLIT, o=QG)
        wide = sb("wide", [P, 1], I32)
        row_max = sb("row_max", [P, QG * TPC], F32)
        gm_rest = sb("gm_rest", [QG * TPC, P], F32)
        gm_parts = sb("gm_parts", [QG * TPC, SPLIT, P], BF16)

        tp = [ps[:, i, :] for i in (0, 1)]
        pj = [ps[:, i, :] for i in (2, 3)]
        vp = ps[:, 4, :]
        am = ps[:, 5:7, 0:2 * (KV + 1)].rearrange("p a (b c) -> p a b c", b=2)
        n2 = ps[:, 7, :]
        sc = [ps[:, UNIT * i:UNIT * i + UNIT, :] for i in range(SLOTS)]
        acc = [ps[:, i, :] for i in (6, 7)]
        tr = [a.rearrange("p (t q r) -> p t q r", t=TPC, q=QG) for a in acc]
        ffn_ps = acc[0]
        ffn_tp = acc[0][:, 0:CH // 2].bitcast(BF16)
        ffn_wtp = acc[1][:, 0:CH // 2].bitcast(BF16)

        x_loaded = [sem(f"x_loaded{i}") for i in range(2)]
        w_loaded = sem("w_loaded")
        small_loaded = sem("small_loaded")
        w8_loaded = sem("w8_loaded")
        zeros_set = sem("zeros_set")
        consts_set = sem("consts_set")
        ones_set = sem("ones_set")
        e_neg_ready = sem("e_neg_ready")
        scal = sem("scal")
        w_turned = sem("w_turned")
        w_copied = sem("w_copied")
        dec = sem("dec")
        wf_turned = sem("wf_turned")
        wf_copied = sem("wf_copied")
        stats_ready = sem("stats_ready")
        moments_ready = sem("moments_ready")
        eps_added = sem("eps_added")
        rstd_ready = sem("rstd_ready")
        xn_ready = sem("xn_ready")
        tp_ready = sem("tp_ready")
        xnT_ready = sem("xnT_ready")
        proj_ready = sem("proj_ready")
        p32_ready = sem("p32_ready")
        part1_ready = sem("part1_ready")
        rest_ready = sem("rest_ready")
        part2_ready = sem("part2_ready")
        part3_ready = sem("part3_ready")
        parts_stored = [sem(f"parts_stored{i}") for i in range(QG + 1)]
        pj_read = sem("pj_read")
        epos_ready = sem("epos_ready")
        sigma_ready = sem("sigma_ready")
        sq_ready = sem("sq_ready")
        n2_ready = sem("n2_ready")
        v_proj_ready = sem("v_proj_ready")
        v_tile_ready = sem("v_tile_ready")
        v_stored = [sem(f"v_stored{i}") for i in range(2)]
        am_ready = sem("am_ready")
        am_used = sem("am_used")
        n2_used = sem("n2_used")
        rnorm_ready = sem("rnorm_ready")
        gd = sem("gd")
        bound_in = sem("bound_in")
        k_mean_ready = sem("k_mean_ready")
        k_mean_norm = sem("k_mean_norm")
        bound_root = sem("bound_root")
        range_ready = sem("range_ready")
        bound_all = sem("bound_all")
        guard_rows_ready = sem("guard_rows_ready")
        wide_ready = sem("wide_ready")
        guard_stored = sem("guard_stored")
        gm_loaded = sem("gm_loaded")
        gm_scores = sem("gm_scores")
        gm_scores_used = sem("gm_scores_used")
        gm_turned = sem("gm_turned")
        gm_step = sem("gm_step")
        gm_split = sem("gm_split")
        gm_stored = sem("gm_stored")
        operands_loaded = [sem(f"operands_loaded{i}") for i in range(2)]
        scores_ready = sem("scores_ready")
        probs_ready = sem("probs_ready")
        pv_done = sem("pv_done")
        oT_ready = sem("oT_ready")
        tr_ready = sem("tr_ready")
        rden_ready = sem("rden_ready")
        head_out_ready = sem("head_out_ready")
        f_moments = sem("f_moments")
        f_eps = sem("f_eps")
        f_rstd = sem("f_rstd")
        f_step = sem("f_step")
        xq_ready = sem("xq_ready")
        xq_turned = sem("xq_turned")
        xqT_ready = sem("xqT_ready")
        ffn_ready = sem("ffn_ready")
        y_ready = sem("y_ready")
        y_stored = sem("y_stored")

        block = ctx.enter_context(nc.Block())

        @block.sync
        def _(sp):
            def load_x(c, par):
                sp.dma_start(resid[:, bass.ds(c * TPC, TPC), :], x_tiles[:, bass.ds(c * TPC, TPC), :])\
                    .then_inc(x_loaded[par], 16)

            for o in range(QG + 1):
                sp.sem_inc(parts_stored[o], 16 * TERMS)
            for par in range(2):
                sp.sem_inc(v_stored[par], 16)
            sp.sem_inc(y_stored, 16)
            sp.sem_inc(gm_stored, 16)

            load_x(0, 0)
            sp.wait_ge(w_loaded, 48)
            load_x(1, 1)
            sp.dma_start(w8[:, :, :], weight.rearrange("(a p) i -> p a i", p=P)).then_inc(w8_loaded, 16)

            def store_parts(c, it, last):
                for par in range(2):
                    if not last:
                        sp.wait_ge(x_loaded[par], 16 * it + 16)
                        load_x(c + par + 2, par)
                    for o in range(QG + 1):
                        sp.wait_ge(part3_ready, (c + par) * (QG + 1) + o + 1)
                        for r in range(TERMS):
                            rows = slice(r * DH, r * DH + DH)
                            if o < QG:
                                dst = q_aug[bass.ds((c + par) * HEADS, HEADS), rows, o * CH:o * CH + CH]
                                src = parts[:, o, Q_PART[r], :]
                            else:
                                dst = k_aug[bass.ds((c + par) * HEADS, HEADS), rows, :]
                                src = parts[:, o, K_PART[r], :]
                            sp.dma_start(dst, src).then_inc(parts_stored[o], 16)
                    sp.wait_ge(v_tile_ready, c + par + 1 + ONE_FREE)
                    sp.dma_start(v_dst(c + par), v_tiles[:, par, :, :, :].rearrange("p h t w -> p h (t w)"))\
                        .then_inc(v_stored[par], 16)

            def v_dst(c):
                return v_aug[bass.ds(c, 1), :, :, :].rearrange("a h p w -> p (a h) w")

            with sp.Fori(0, NG // 2 - 1) as it:
                store_parts(2 * it, it, False)
            store_parts(NG - 2, NG // 2 - 1, True)

            def load_qk(n, g, h, par, done):
                sp.dma_start(q_st[0:ROWS, par, :], q_aug[bass.ds(n, 1), :, :].rearrange("a r s -> (a r) s"))\
                    .then_inc(done, 16)
                b4 = (g // CPB) * CPB
                sp.dma_start(k_st[0:ROWS, par, :].rearrange("r (c s) -> r c s", c=CPB), k_src(b4, h)).then_inc(done, 16)

            def k_src(b4, h):
                return k_aug[bass.ds(b4 * HEADS, CPB * HEADS), :, :]\
                    .rearrange("(c h) r s -> h r c s", c=CPB)[h, :, :, :]

            def load_v(g, h, par):
                sp.dma_start(v_st[:, par, :, :].rearrange("p (c t) w -> p c (t w)", c=CPB), v_src((g // CPB) * CPB, h))\
                    .then_inc(operands_loaded[par], 16)

            def v_src(b4, h):
                return v_aug[bass.ds(b4, CPB), h, :, :].rearrange("c p w -> p c w")

            def load_guard(n, par):
                sp.dma_start(q_st[ROWS:AUG, par, :], guard[bass.ds(n, 1), :, :].rearrange("a i s -> (a i) s"))\
                    .then_inc(operands_loaded[par], 16)

            for o in range(QG + 1):
                sp.wait_ge(parts_stored[o], 16 * TERMS * (NG + 1))
            for h in range(2):
                load_qk(h, 0, h, h, operands_loaded[h])
            sp.wait_ge(guard_rows_ready, BATCH * SPLIT)
            for b in range(BATCH):
                rows = guard_rows[0:P:DH, b, :, :, :].rearrange("p i o s -> p (i o s)")
                sp.dma_start(guard[b * CPB * HEADS:(b + 1) * CPB * HEADS, :, :].rearrange("(c h) i s -> h c (i s)", c=CPB),
                             rows.unsqueeze(1).to_broadcast([HEADS, CPB, SPLIT * QG * CH])).then_inc(guard_stored, 16)
            for par in range(2):
                sp.wait_ge(v_stored[par], 16 * (NG // 2 + 1))
            for h in range(2):
                load_v(0, h, h)
            sp.wait_ge(guard_stored, 16 * BATCH)

            sp.wait_ge(wide_ready, 1)
            bound_too_wide = sp.value_load(wide[0:1, 0:1], min_val=0, max_val=1)
            with sp.If(bound_too_wide):
                sp.wait_ge(operands_loaded[0], 48)
                with sp.Fori(0, NG) as g:
                    for h in range(HEADS):
                        n = g * HEADS + h
                        sp.wait_ge(gm_stored, 16 * n + 16)
                        load_qk(n, g, h, 0, gm_loaded)
                        sp.wait_ge(gm_split, n + 1)
                        sp.dma_start(guard[bass.ds(n, 1), :, :].rearrange("a i (u p) -> u (a i) p", p=P),
                                     gm_parts[:, :, :]).then_inc(gm_stored, 16)
                sp.wait_ge(gm_stored, 16 * (NG * HEADS + 1))
                load_qk(0, 0, 0, 0, gm_loaded)
                sp.wait_ge(gm_loaded, 32 * (NG * HEADS + 1))

            def load_block(g, h):
                n = g * HEADS + h
                par = h % 2
                if not (isinstance(g, int) and g == 0 and h < 2):
                    sp.wait_ge(pv_done, (n - 1) * ST)
                    load_qk(n, g, h, par, operands_loaded[par])
                    load_v(g, h, par)
                load_guard(n, par)

            for h in range(HEADS):
                load_block(0, h)
            with sp.Fori(1, NG) as g:
                for h in range(HEADS // 2):
                    load_block(g, h)
                sp.wait_ge(y_ready, g * TPC + ONE_FREE)
                sp.dma_start(out_tiles[:, bass.ds((g - 1) * TPC, TPC), :], y_out[:, :, :]).then_inc(y_stored, 16)
                for h in range(HEADS // 2, HEADS):
                    load_block(g, h)
            sp.wait_ge(y_ready, NG * TPC + ONE_FREE)
            sp.dma_start(out_tiles[:, NT - TPC:NT, :], y_out[:, :, :]).then_inc(y_stored, 16)
            sp.wait_ge(y_stored, 16 * (NG + 1))

        @block.gpsimd
        def _(pool_e):
            pool_e.memset(ident[:, :], 0.0).then_inc(zeros_set, 1)
            pool_e.memset(ident_bf[:, :], 0.0).then_inc(zeros_set, 1)
            pool_e.memset(head_ones[:, :], 1.0).then_inc(zeros_set, 1)
            pool_e.wait_ge(zeros_set, 3)
            for m in (ident, ident_bf):
                pool_e.affine_select(out=m[:, :], in_=m[:, :], compare_op=ALU.not_equal, fill=1.0, base=0,
                                     pattern=[[-1, P]], channel_multiplier=1).then_inc(consts_set, 1)
            blocks = head_ones[:, :].rearrange("p (a b) -> p a b", b=DH)
            pool_e.affine_select(out=blocks, in_=blocks, compare_op=ALU.is_ge, fill=0.0, base=0,
                                 pattern=[[-DH, HEADS], [0, DH]], channel_multiplier=1).then_inc(zeros_set, 1)
            pool_e.wait_ge(zeros_set, 4)
            pool_e.affine_select(out=blocks, in_=blocks, compare_op=ALU.is_ge, fill=0.0, base=DH - 1,
                                 pattern=[[DH, HEADS], [0, DH]], channel_multiplier=-1).then_inc(consts_set, 1)
            pool_e.memset(minus_half[:, :], -0.5).then_inc(consts_set, 1)
            pool_e.memset(half[:, :], 0.5).then_inc(consts_set, 1)
            pool_e.memset(eps[:, :], LN_EPS).then_inc(consts_set, 1)
            pool_e.memset(v_tiles[:, :, :, :, DH:VW], 0.0).then_inc(zeros_set, 1)
            pool_e.wait_ge(zeros_set, 5)
            pool_e.memset(v_tiles[:, :, :, :, DH:DH + 1], 1.0).then_inc(ones_set, 1)
            pool_e.memset(ones_row[:, :], 1.0).then_inc(ones_set, 1)
            pool_e.wait_ge(ones_set, 2)
            pool_e.memset(k_st[ROWS:P, :, :], 1.0).then_inc(ones_set, 1)
            pool_e.wait_ge(consts_set, 6)
            pool_e.wait_ge(ones_set, 3)

            def rstd_of(c, par):
                pool_e.wait_ge(moments_ready, c + 1)
                pool_e.tensor_tensor(var_eps[:, :], moments[:, par, :, 1], eps[:, :], ALU.add)\
                    .then_inc(eps_added, 1)
                pool_e.wait_ge(eps_added, c + 1)
                pool_e.tensor_tensor(rstd[:, par, :], var_eps[:, :], minus_half[:, :], ALU.pow).then_inc(rstd_ready, 1)

            def chunk(c, par, last):
                for o in range(QG + 1):
                    if o == 2 and not last:
                        pool_e.wait_ge(sq_ready, c * (QG + 1) + o)
                        rstd_of(c + 1, 1 - par)
                        pool_e.wait_ge(rstd_ready, c + 2)
                    i = c * (QG + 1) + o
                    slot = (par * (QG + 1) + o) % 2
                    pool_e.wait_ge(part1_ready, i + 1)
                    pool_e.wait_ge(n2_ready, i)
                    pool_e.tensor_tensor(sq[:, slot, :], parts[:, o, 0, :], parts[:, o, 0, :], ALU.mult)\
                        .then_inc(sq_ready, 1)

            rstd_of(0, 0)
            pool_e.wait_ge(rstd_ready, 1)
            chunk(0, 0, False)
            chunk(1, 1, False)
            with pool_e.Fori(1, NG // 2 - 1) as it:
                chunk(2 * it, 0, False)
                chunk(2 * it + 1, 1, False)
            chunk(NG - 2, 0, False)
            chunk(NG - 1, 1, True)

            pool_e.wait_ge(sq_ready, NG * (QG + 1))
            pool_e.wait_ge(bound_in, 2)
            pool_e.tensor_tensor(bound[:, 4:6, :], bound[:, 2:4, :], half[:, :].rearrange("p (a b) -> p a b", a=2), ALU.pow)\
                .then_inc(bound_root, 1)
            pool_e.wait_ge(range_ready, 1)
            pool_e.partition_all_reduce(range_all[:, :], bound[:, 6, :], P, MAX_OVER_PARTITIONS).then_inc(bound_all, 1)
            pool_e.wait_ge(bound_all, 1)

            with pool_e.Fori(0, NG) as g:
                pool_e.wait_ge(f_moments, g + 1)
                pool_e.tensor_tensor(var_eps[:, :], moments[:, 0, :, 1], eps[:, :], ALU.add).then_inc(f_eps, 1)
                pool_e.wait_ge(f_eps, g + 1)
                pool_e.tensor_tensor(rstd[:, 0, :], var_eps[:, :], minus_half[:, :], ALU.pow).then_inc(f_rstd, 1)
                pool_e.wait_ge(f_rstd, g + 1)

        @block.scalar
        def _(act):
            act.dma_start(wq_raw[:, :, :], Wq.rearrange("(a p) i -> p a i", p=P)).then_inc(w_loaded, 16)
            act.dma_start(wkv_raw[:, 0, :], Wk).then_inc(w_loaded, 16)
            act.dma_start(wkv_raw[:, 1, :], Wv).then_inc(w_loaded, 16)
            act.dma_start(mem_w, memory_weight.partition_broadcast(P)).then_inc(small_loaded, 16)
            act.dma_start(ws_col, weight_scale.partition_broadcast(P)).then_inc(small_loaded, 16)
            act.dma_start(s_raw[:, :], input_scale.partition_broadcast(P)).then_inc(small_loaded, 16)
            act.dma_start(mem_aug[:, 0:KV], memory).then_inc(small_loaded, 16)
            act.dma_start(mem_aug[:, KV:KV + 1], memory_norm).then_inc(small_loaded, 16)
            act.sem_inc(xnT_ready, TWO_FREE)
            act.sem_inc(p32_ready, TWO_FREE)
            act.sem_inc(pj_read, ONE_FREE)
            act.sem_inc(v_tile_ready, ONE_FREE)
            act.sem_inc(probs_ready, THREE_FREE)
            act.wait_ge(small_loaded, 80)
            act.activation(e_neg, mem_w, ACT.Exp, scale=-1.0).then_inc(e_neg_ready, 1)
            for j in range(3 * KT // 2):
                act.wait_ge(w_turned, j + 1)
                if j < KT:
                    dst, src = wqT[:, j, :], tp[j % 2]
                else:
                    dst = (wkT, wvT)[j - KT][:, :, :].rearrange("p k o -> p (k o)")
                    src = tp[j % 2]
                act.activation(dst, src, ACT.Copy).then_inc(w_copied, 1)

            def copy_xnT(c, par, ks, first=False):
                if not first:
                    act.wait_ge(v_proj_ready, c)
                for k in ks:
                    act.wait_ge(tp_ready, c * KT + k + 1)
                    act.activation(xnT[:, par, k, :], tp[k % 2], ACT.Copy).then_inc(xnT_ready, 1)

            def exp_neg(c, par, o):
                act.wait_ge(pj_read, c * QG + o + 1 + ONE_FREE)
                act.activation(epos[:, o % 2, :], neg[:, o % 2, :], ACT.Exp, scale=-1.0).then_inc(epos_ready, 1)

            def second_part(c, par, o):
                act.wait_ge(rest_ready, c * (QG + 1) + o + 1 + TWO_FREE)
                act.activation(parts[:, o, 1, :], r32[:, (par * (QG + 1) + o) % 2, :], ACT.Copy).then_inc(part2_ready, 1)

            def chunk(c, par, last):
                for o in range(QG + 1):
                    i = c * (QG + 1) + o
                    slot = (par * (QG + 1) + o) % 2
                    act.wait_ge(proj_ready, i + 1)
                    act.wait_ge(rest_ready, i + 1)
                    act.activation(p32[:, slot, :], pj[slot], ACT.Copy).then_inc(p32_ready, 1)
                    if o < QG:
                        act.wait_ge(sigma_ready, c * QG + o + 1)
                        act.activation(relu[:, o % 2, :], pj[slot], ACT.Relu)
                        act.activation(neg[:, o % 2, :], pj[slot], ACT.Relu, scale=-1.0).then_inc(pj_read, 1)
                    if o >= 1:
                        exp_neg(c, par, o - 1)
                        second_part(c, par, o - 1)
                if not last:
                    copy_xnT(c + 1, 1 - par, range(KT // 2))
                second_part(c, par, QG)
                act.wait_ge(v_proj_ready, c + 1 + ONE_FREE)
                act.wait_ge(v_stored[par], (c - par) * 8 + 16)
                act.wait_ge(scal, 4)
                act.activation(v_tiles[:, par, :, :, 0:DH], vp.rearrange("p (t h d) -> p h t d", t=TPC, h=HEADS),
                               ACT.Copy, scale=w_dot).then_inc(v_tile_ready, 1)
                if not last:
                    copy_xnT(c + 1, 1 - par, range(KT // 2, KT))

            copy_xnT(0, 0, range(KT), first=True)
            with act.Fori(0, NG // 2 - 1) as it:
                chunk(2 * it, 0, False)
                chunk(2 * it + 1, 1, False)
            chunk(NG - 2, 0, False)
            chunk(NG - 1, 1, True)
            with act.Fori(0, NG * HEADS // 2) as pair:
                for v in range(2 * UNITS):
                    act.wait_ge(scores_ready, pair * (2 * UNITS) + v + 1)
                    act.activation(probs[:, v % PSLOTS, :],
                                   sc[v % UNITS % SLOTS][:, :, :].rearrange("p a b -> p (a b)"), ACT.Exp,
                                   scale=SCALE).then_inc(probs_ready, 1)

        @block.tensor
        def _(pe):
            pe.sem_inc(v_proj_ready, ONE_FREE)
            pe.wait_ge(consts_set, 6)
            pe.wait_ge(w_loaded, 48)
            for j in range(KT + 2):
                if j >= 2:
                    pe.wait_ge(w_copied, j - 1)
                for a in range(KT):
                    src = wq_raw[:, a, j * P:j * P + P] if j < KT else wkv_raw[:, j - KT, a * P:a * P + P]
                    last = pe.transpose(tp[j % 2][:, a * P:a * P + P], src, ident[:, :])
                last.then_inc(w_turned, 1)
            pe.wait_ge(w_copied, KT + 2)

            def turn_xn(c, ks):
                pe.wait_ge(xn_ready, c + 1)
                for k in ks:
                    pe.wait_ge(xnT_ready, c * KT + k + 1)
                    for t in range(TPC):
                        last = pe.transpose(tp[k % 2][:, t * P:t * P + P], xn[:, t, k * P:k * P + P], ident[:, :])
                    last.then_inc(tp_ready, 1)

            def norms(c, par, o):
                i = c * (QG + 1) + o
                pe.wait_ge(sq_ready, i + 1)
                pe.wait_ge(n2_used, i + 1)
                pe.matmul(n2, head_ones[:, :], sq[:, (par * (QG + 1) + o) % 2, :], start=True, stop=True)\
                    .then_inc(n2_ready, 1)

            def memory_products(c, q):
                pe.wait_ge(sigma_ready, c * QG + q + 1 + TWO_FREE)
                pe.wait_ge(am_used, c * QG + q + ONE_FREE)
                for t in range(TPC):
                    last = pe.matmul(am[:, t // 2, t % 2, :], sigma[:, q, t * P:t * P + P], mem_aug[:, :],
                                     start=True, stop=True)
                last.then_inc(am_ready, 1)

            def chunk(c, par, first_chunk=False, last_chunk=False):
                for o in range(QG + 1):
                    if o == 1:
                        pe.wait_ge(p32_ready, c * (QG + 1) + TWO_FREE)
                    else:
                        pe.wait_ge(pj_read, c * QG + max(o - 1, 0) + ONE_FREE)
                    for k in range(KT):
                        if o == 0:
                            pe.wait_ge(xnT_ready, c * KT + k + 1 + TWO_FREE)
                        w = wqT[:, k, o * P:o * P + P] if o < QG else wkT[:, k, :]
                        last = pe.matmul(pj[(par * (QG + 1) + o) % 2], w, xnT[:, par, k, :],
                                         start=(k == 0), stop=(k == KT - 1))
                    last.then_inc(proj_ready, 1)
                    if o >= 1:
                        norms(c, par, o - 1)
                    if not first_chunk and o < QG:
                        memory_products(c - 1, o)
                if not last_chunk:
                    turn_xn(c + 1, range(KT // 2))
                pe.wait_ge(v_tile_ready, c + 1)
                for t in range(TPC):
                    for k in range(KT):
                        last = pe.matmul(vp[:, t * P:t * P + P], xnT[:, par, k, t * P:t * P + P], wvT[:, k, :],
                                         start=(k == 0), stop=(k == KT - 1))
                last.then_inc(v_proj_ready, 1)
                norms(c, par, QG)
                if not last_chunk:
                    turn_xn(c + 1, range(KT // 2, KT))

            turn_xn(0, range(KT))
            pe.wait_ge(scal, 4)
            chunk(0, 0, first_chunk=True)
            chunk(1, 1)
            with pe.Fori(1, NG // 2 - 1) as it:
                chunk(2 * it, 0)
                chunk(2 * it + 1, 1)
            chunk(NG - 2, 0)
            chunk(NG - 1, 1, last_chunk=True)

            pe.wait_ge(k_mean_ready, 1)
            pe.matmul(n2[:, 0:BATCH], head_ones[:, :], k_mean_sq[:, :], start=True, stop=True).then_inc(k_mean_norm, 1)
            for q in range(QG):
                memory_products(NG - 1, q)
            pe.wait_ge(am_used, NG * QG + ONE_FREE)

            pe.wait_ge(wide_ready, 1)
            bound_too_wide = pe.value_load(wide[0:1, 0:1], min_val=0, max_val=1)
            with pe.If(bound_too_wide):
                with pe.Fori(0, NG * HEADS) as n:
                    pe.wait_ge(gm_loaded, n * 32 + 32)
                    for u in range(QG * TPC):
                        pe.wait_ge(gm_scores_used, n * (QG * TPC) + u + ONE_FREE)
                        for c4 in range(CPB):
                            last = pe.matmul(ps[:, c4, :], q_st[0:ROWS, 0, u * P:u * P + P],
                                             k_st[0:ROWS, 0, c4 * CH:c4 * CH + CH], start=True, stop=True)
                        last.then_inc(gm_scores, 1)
                    pe.wait_ge(gm_scores_used, n * (QG * TPC) + QG * TPC + ONE_FREE)
                    pe.transpose(ps[0:QG * TPC, 6, 0:P], row_max[:, :], ident[:, :]).then_inc(gm_turned, 1)

            def scores(n, par, u):
                pe.wait_ge(probs_ready, n * UNITS + u - units_since(u) + 1 + THREE_FREE)
                for x in range(UNIT):
                    j, q = divmod(UNIT * u + x, QG)
                    last = pe.matmul(sc[u % SLOTS][:, x, :], k_st[0:AUG, par, j * P:j * P + P],
                                     q_st[0:AUG, par, q * CH:q * CH + CH], start=True, stop=True)
                last.then_inc(scores_ready, 1)

            def weigh_v(n, par, u):
                if u % UNITS_OF_TILE == UNITS_OF_TILE - 1:
                    j = u // UNITS_OF_TILE
                    for q in range(QG):
                        v, x = divmod(QG * j + q, UNIT)
                        last = pe.matmul(acc[par][VW * q:VW * q + VW, :], v_st[:, par, j, :],
                                         probs[:, (par * UNITS + v) % PSLOTS, x * CH:x * CH + CH],
                                         start=(j == 0), stop=(j == ST - 1))
                    last.then_inc(pv_done, 1)

            def turn_out(n, par):
                pe.wait_ge(oT_ready, n + 1)
                for t in range(TPC):
                    last = pe.transpose(acc[par][:, t * P:t * P + P], oT[:, par, t * P:t * P + P], ident[:, :])
                last.then_inc(tr_ready, 1)

            def ffn_turn(g, t):
                if t == 0:
                    pe.wait_ge(xq_ready, g + 1)
                pe.wait_ge(y_ready, g * TPC + t + ONE_FREE)
                for k in range(KT):
                    last = pe.transpose(ffn_tp[:, k * P:k * P + P], xq[:, t, k * P:k * P + P], ident_bf[:, :])
                last.then_inc(xq_turned, 1)

            def ffn_product(g, t):
                pe.wait_ge(xqT_ready, g * TPC + t + 1)
                for k in range(KT):
                    last = pe.matmul(ffn_ps, xqT[:, k, :], wT_ffn[:, k, :], start=(k == 0), stop=(k == KT - 1))
                last.then_inc(ffn_ready, 1)

            def turn_ffn_weight(k):
                pe.wait_ge(dec, 8)
                pe.wait_ge(wf_copied, k)
                for a in range(KT):
                    last = pe.transpose(ffn_wtp[:, a * P:a * P + P], w_val[:, a, k * P:k * P + P], ident_bf[:, :])
                last.then_inc(wf_turned, 1)

            def pair(n0, trip, first=False, ffn_g=None, ffn_read=None):
                for par in range(2):
                    n = n0 + par
                    pe.wait_ge(operands_loaded[par], trip * 64 + 64)
                    for u in range(UNITS):
                        scores(n, par, u)
                        if u >= SLOTS:
                            if u == SLOTS:
                                pe.wait_ge(head_out_ready, n + 1)
                                if first and par == 1:
                                    pe.wait_ge(wf_copied, KT)
                                if ffn_read is not None and par == 0:
                                    pe.wait_ge(y_ready, ffn_read)
                            weigh_v(n, par, u - SLOTS)
                        elif not (first and par == 0):
                            weigh_v(n - 1, 1 - par, UNITS + u - SLOTS)
                        if first and par == 0:
                            if u >= W_TURN_AT and (u - W_TURN_AT) % 3 == 0:
                                turn_ffn_weight((u - W_TURN_AT) // 3)
                        elif u == TURN_AT:
                            turn_out(n - 1, 1 - par)
                        if ffn_g is not None and par == 1 and u in FFN_AT:
                            step = FFN_AT.index(u)
                            if step == 0:
                                pe.wait_ge(head_out_ready, n + TWO_FREE)
                            (ffn_turn, ffn_product)[step % 2](ffn_g, step // 2)

            pairs = HEADS // 2
            pair(0, 0, first=True)
            with pe.Fori(1, pairs) as hp:
                pair(2 * hp, hp)
            with pe.Fori(1, NG) as g:
                pair(g * HEADS, g * pairs, ffn_g=g - 1)
                with pe.Fori(1, pairs) as hp:
                    pair(g * HEADS + 2 * hp, g * pairs + hp, ffn_read=g * TPC + ONE_FREE)
            last_n = NG * HEADS - 1
            for u in range(UNITS - SLOTS, UNITS):
                pe.wait_ge(probs_ready, last_n * UNITS + u + 1 + THREE_FREE)
                weigh_v(last_n, 1, u)
            turn_out(last_n, 1)
            for t in range(TPC):
                ffn_turn(NG - 1, t)
                ffn_product(NG - 1, t)

        @block.vector
        def _(dve):
            dve.sem_inc(rest_ready, TWO_FREE)
            dve.sem_inc(sigma_ready, TWO_FREE)
            dve.sem_inc(am_used, ONE_FREE)
            dve.sem_inc(head_out_ready, TWO_FREE)
            dve.sem_inc(n2_used, ONE_FREE)
            dve.sem_inc(gm_scores_used, ONE_FREE)
            dve.sem_inc(y_ready, ONE_FREE)

            def statistics(c):
                for t in range(TPC):
                    last = dve.bn_stats(stats[:, t, :], resid[:, bass.ds(c * TPC + t, 1), :].rearrange("p a d -> p (a d)"))
                last.then_inc(stats_ready, 1)

            def mean_and_variance(par):
                for t in range(TPC):
                    last = dve.bn_aggr(moments[:, par, t, :], stats[:, t, :])
                last.then_inc(moments_ready, 1)

            def normalise(c, par):
                dve.wait_ge(rstd_ready, c + 1)
                dve.wait_ge(tp_ready, c * KT)
                for t in range(TPC):
                    last = dve.tensor_scalar(xn[:, t, :], resid[:, bass.ds(c * TPC + t, 1), :].rearrange("p a d -> p (a d)"),
                                             moments[:, par, t, 0:1], rstd[:, par, t:t + 1], ALU.subtract, ALU.mult)
                last.then_inc(xn_ready, 1)

            dve.wait_ge(x_loaded[0], 16)
            statistics(0)
            dve.wait_ge(stats_ready, 1)
            mean_and_variance(0)
            normalise(0, 0)
            dve.wait_ge(e_neg_ready, 1)
            dve.tensor_scalar(one_plus, e_neg, 1.0, None, ALU.add).then_inc(scal, 1)
            dve.wait_ge(scal, 1)
            dve.reciprocal(w_mem, one_plus).then_inc(scal, 1)
            dve.wait_ge(scal, 2)
            dve.tensor_scalar(w_dot, w_mem, -1.0, 1.0, ALU.mult, ALU.add).then_inc(scal, 1)
            dve.tensor_scalar(mem_aug[:, 0:KV], mem_aug[:, 0:KV], w_mem, None, ALU.mult).then_inc(scal, 1)
            dve.tensor_copy(s_col, s_raw[:, :]).then_inc(scal, 1)
            dve.wait_ge(scal, 5)
            dve.reciprocal(inv_s, s_col).then_inc(scal, 1)
            dve.tensor_tensor(sw, s_col, ws_col, ALU.mult).then_inc(scal, 1)

            def finish(c, par, o):
                i = c * (QG + 1) + o
                slot = (par * (QG + 1) + o) % 2
                dve.wait_ge(part2_ready, i + 1)
                dve.tensor_tensor(parts[:, o, 2, :], r32[:, slot, :], parts[:, o, 1, :], ALU.subtract)\
                    .then_inc(part3_ready, 1)
                if o < QG:
                    dve.wait_ge(epos_ready, c * QG + o + 1)
                    dve.scalar_tensor_tensor(sigma[:, o, :], epos[:, o % 2, :], -1.0, relu[:, o % 2, :],
                                             ALU.add, ALU.add).then_inc(sigma_ready, 1)
                dve.wait_ge(n2_ready, i + 1)
                dve.tensor_reduce(norm2[:, bass.ds(c, 1), o], n2, AX.X, ALU.max).then_inc(n2_used, 1)

            def memory_part(c, q):
                dve.wait_ge(am_ready, c * QG + q + 1)
                dve.reciprocal(rnorm[:, :, :], am[:, :, :, KV]).then_inc(rnorm_ready, 1)
                dve.wait_ge(rnorm_ready, c * QG + q + 1)
                for t in range(TPC):
                    row = resid[:, bass.ds(c * TPC + t, 1), q * KV:q * KV + KV].rearrange("p a d -> p (a d)")
                    last = dve.scalar_tensor_tensor(row, am[:, t // 2, t % 2, 0:KV], rnorm[:, t // 2, t % 2:t % 2 + 1], row,
                                                    ALU.mult, ALU.add)
                last.then_inc(am_used, 1)

            def chunk(c, par, first_chunk=False, last_chunk=False):
                for o in range(QG + 1):
                    i = c * (QG + 1) + o
                    slot = (par * (QG + 1) + o) % 2
                    if o == 1 and not last_chunk:
                        dve.wait_ge(stats_ready, c + 2)
                    dve.wait_ge(p32_ready, i + 1 + TWO_FREE)
                    dve.wait_ge(parts_stored[o], (c + 1) * (16 * TERMS))
                    dve.tensor_copy(parts[:, o, 0, :], p32[:, slot, :]).then_inc(part1_ready, 1)
                    if o == 1 and not last_chunk:
                        mean_and_variance(1 - par)
                    if o == QG:
                        dve.tensor_reduce(k_sum[:, bass.ds(c, 1)], p32[:, slot, :], AX.X, ALU.add)
                    if o == 0 and not last_chunk:
                        dve.wait_ge(x_loaded[1 - par], (c + par) * 8 + 16)
                    dve.wait_ge(part1_ready, i + 1)
                    dve.tensor_tensor(r32[:, slot, :], p32[:, slot, :], parts[:, o, 0, :], ALU.subtract)\
                        .then_inc(rest_ready, 1)
                    if o >= 1:
                        finish(c, par, o - 1)
                    if not first_chunk and o < QG:
                        memory_part(c - 1, o)
                    if o == 0 and not last_chunk:
                        statistics(c + 1)
                    if o == 2 and not last_chunk:
                        normalise(c + 1, 1 - par)
                finish(c, par, QG)

            chunk(0, 0, first_chunk=True)
            chunk(1, 1)
            with dve.Fori(1, NG // 2 - 1) as it:
                chunk(2 * it, 0)
                chunk(2 * it + 1, 1)
            chunk(NG - 2, 0)
            chunk(NG - 1, 1, last_chunk=True)

            dve.wait_ge(n2_used, NG * (QG + 1) + ONE_FREE)
            by_batch = norm2[:, :, :].rearrange("p (b c) o -> p b c o", b=BATCH)
            dve.tensor_reduce(k_total[:, :], k_sum[:, :].rearrange("p (b c) -> p b c", b=BATCH), AX.X, ALU.add).then_inc(gd, 1)
            dve.tensor_reduce(bound[:, 0, :], by_batch[:, :, :, 0:QG], AX.XY, ALU.max).then_inc(gd, 1)
            dve.tensor_reduce(bound[:, 1, :], by_batch[:, :, :, QG], AX.X, ALU.max).then_inc(gd, 1)
            dve.wait_ge(gd, 1)
            dve.scalar_tensor_tensor(k_mean_sq[:, :], k_total[:, :], 1.0 / SEQ ** 2, k_total[:, :], ALU.mult, ALU.mult)\
                .then_inc(k_mean_ready, 1)
            dve.wait_ge(gd, 3)
            dve.tensor_tensor(bound[:, 2, :], bound[:, 0, :], bound[:, 1, :], ALU.mult).then_inc(bound_in, 1)
            dve.wait_ge(k_mean_norm, 1)
            dve.tensor_tensor(bound[:, 3, :], bound[:, 0, :], n2[:, 0:BATCH], ALU.mult).then_inc(bound_in, 1)
            dve.wait_ge(bound_root, 1)
            dve.tensor_tensor(bound[:, 6, :], bound[:, 4, :], bound[:, 5, :], ALU.add).then_inc(range_ready, 1)
            dve.tensor_tensor(bound[:, 7, :], bound[:, 4, :], bound[:, 5, :], ALU.subtract).then_inc(gd, 1)
            dve.wait_ge(gd, 4)
            dve.tensor_scalar(bound[:, 8, :], bound[:, 7, :], -GUARD_MARGIN / 2, GUARD_OFFSET, ALU.mult, ALU.add).then_inc(gd, 1)
            dve.wait_ge(gd, 5)
            dve.tensor_copy(guard_bf[:, :, 0], bound[:, 8, :]).then_inc(gd, 1)
            dve.wait_ge(gd, 6)
            dve.tensor_tensor(guard_rest[:, :], bound[:, 8, :], guard_bf[:, :, 0], ALU.subtract).then_inc(gd, 1)
            dve.wait_ge(gd, 7)
            dve.tensor_copy(guard_bf[:, :, 1], guard_rest[:, :]).then_inc(gd, 1)
            dve.wait_ge(gd, 8)
            dve.tensor_tensor(guard_bf[:, :, 2], guard_rest[:, :], guard_bf[:, :, 1], ALU.subtract).then_inc(gd, 1)
            dve.wait_ge(gd, 9)
            dve.tensor_copy(guard_parts[:, :, :], guard_bf[:, :, :]).then_inc(gd, 1)
            dve.wait_ge(gd, 10)
            dve.wait_ge(ones_set, 3)
            for b in range(BATCH):
                for i in range(SPLIT):
                    dve.tensor_scalar(guard_rows[:, b, i, :, :], ones_row[:, :].unsqueeze(1).to_broadcast([P, QG, CH]),
                                      guard_parts[:, b, i:i + 1], None, ALU.mult).then_inc(guard_rows_ready, 1)
            dve.wait_ge(bound_all, 1)
            dve.tensor_reduce(widest[:, :], range_all[:, :], AX.X, ALU.max).then_inc(gd, 1)
            dve.wait_ge(gd, 11)
            dve.tensor_scalar(wide[:, :], widest[:, :], GUARD_LIMIT, None, ALU.is_gt).then_inc(wide_ready, 1)
            for q in range(QG):
                memory_part(NG - 1, q)
            dve.wait_ge(wide_ready, 1)
            bound_too_wide = dve.value_load(wide[0:1, 0:1], min_val=0, max_val=1)
            with dve.If(bound_too_wide):
                with dve.Fori(0, NG * HEADS) as n:
                    for u in range(QG * TPC):
                        dve.wait_ge(gm_scores, n * (QG * TPC) + u + 1)
                        dve.tensor_reduce(row_max[:, u:u + 1], ps[:, 0:CPB, :], AX.XY, ALU.max).then_inc(gm_scores_used, 1)
                    dve.wait_ge(gm_turned, n + 1)
                    turned = ps[0:QG * TPC, 6, 0:P]
                    dve.tensor_scalar(gm_parts[:, 0, :], turned, -1.0, None, ALU.mult).then_inc(gm_step, 1)
                    dve.wait_ge(gm_step, n * 3 + 1)
                    dve.scalar_tensor_tensor(gm_rest[:, :], turned, -1.0, gm_parts[:, 0, :], ALU.mult, ALU.subtract)\
                        .then_inc(gm_step, 1)
                    dve.wait_ge(gm_step, n * 3 + 2)
                    dve.tensor_copy(gm_parts[:, 1, :], gm_rest[:, :]).then_inc(gm_step, 1)
                    dve.wait_ge(gm_step, n * 3 + 3)
                    dve.tensor_tensor(gm_parts[:, 2, :], gm_rest[:, :], gm_parts[:, 1, :], ALU.subtract).then_inc(gm_split, 1)

            dve.wait_ge(w8_loaded, 16)
            mag, sign, twice = work[:, 0:4, :], work[:, 4:8, :], y_out[:, :, :]
            dve.tensor_copy(mag, w8[:, :, :].bitcast(U8)).then_inc(dec, 1)
            dve.wait_ge(dec, 1)
            dve.tensor_scalar(sign, mag, 128.0, 128.0, ALU.is_ge, ALU.mult).then_inc(dec, 1)
            dve.wait_ge(dec, 2)
            dve.tensor_tensor(mag, mag, sign, ALU.subtract).then_inc(dec, 1)
            dve.wait_ge(dec, 3)
            dve.tensor_scalar(mag.bitcast(I32), mag, 960.0, 2.0 ** 20, ALU.add, ALU.mult).then_inc(dec, 1)
            dve.wait_ge(dec, 4)
            dve.tensor_scalar(twice, mag, 2.0, -2.0 ** -6, ALU.mult, ALU.add).then_inc(dec, 1)
            dve.wait_ge(dec, 5)
            dve.tensor_tensor(mag, mag, twice, ALU.min).then_inc(dec, 1)
            dve.tensor_scalar(sign, sign, -2.0 / 128.0, 1.0, ALU.mult, ALU.add).then_inc(dec, 1)
            dve.wait_ge(dec, 7)
            dve.tensor_tensor(w_val[:, :, :], mag, sign, ALU.mult).then_inc(dec, 1)
            for k in range(KT):
                dve.wait_ge(wf_turned, k + 1)
                dve.tensor_copy(wT_ffn[:, k, :], ffn_wtp).then_inc(wf_copied, 1)

            def add_head(n, par, g, h):
                dve.wait_ge(pv_done, n * ST + ST)
                dve.tensor_copy(oT[:, par, :], acc[par]).then_inc(oT_ready, 1)
                dve.wait_ge(tr_ready, n + 1)
                dve.reciprocal(rden[:, :, :], tr[par][:, :, :, DH]).then_inc(rden_ready, 1)
                dve.wait_ge(rden_ready, n + 1)
                dve.tensor_tensor(head_out[:, :, :, :], tr[par][:, :, :, 0:DH],
                                  rden[:, :, :].unsqueeze(3).to_broadcast([P, TPC, QG, DH]), ALU.mult)\
                    .then_inc(head_out_ready, 1)
                dve.wait_ge(head_out_ready, n + 1 + TWO_FREE)
                cols = resid[:, bass.ds(g * TPC, TPC), :].rearrange("p t (q f) -> p t q f", q=QG)[:, :, :, bass.ds(h * DH, DH)]
                dve.tensor_tensor(cols, cols, head_out[:, :, :, :], ALU.add)

            def round_to_float8(g):
                dve.drain()
                for t in range(TPC):
                    dve.bn_stats(stats[:, t, :], resid[:, bass.ds(g * TPC + t, 1), :].rearrange("p a d -> p (a d)"))
                dve.drain()
                for t in range(TPC):
                    last = dve.bn_aggr(moments[:, 0, t, :], stats[:, t, :])
                last.then_inc(f_moments, 1)
                dve.wait_ge(f_rstd, g + 1)
                dve.tensor_scalar(rstd_s[:, :], rstd[:, 0, :], inv_s, None, ALU.mult).then_inc(f_step, 1)
                dve.wait_ge(f_step, g * 6 + 1)
                xs, big = work[:, 0:4, :], work[:, 4:8, :]
                for t in range(TPC):
                    last = dve.tensor_scalar(work[:, t, :], resid[:, bass.ds(g * TPC + t, 1), :].rearrange("p a d -> p (a d)"),
                                             moments[:, 0, t, 0:1], rstd_s[:, t:t + 1], ALU.subtract, ALU.mult)
                last.then_inc(f_step, 1)
                dve.wait_ge(f_step, g * 6 + 2)
                dve.tensor_scalar(xs, xs, FP8_MAX, -FP8_MAX, ALU.min, ALU.max).then_inc(f_step, 1)
                dve.wait_ge(f_step, g * 6 + 3)
                dve.tensor_scalar(big.bitcast(I32), xs.bitcast(I32), 0x7F800000, None, ALU.bitwise_and).then_inc(f_step, 1)
                dve.wait_ge(f_step, g * 6 + 4)
                dve.tensor_scalar(big, big, 2.0 ** -6, 1.5 * 2.0 ** 20, ALU.max, ALU.mult).then_inc(f_step, 1)
                dve.wait_ge(f_step, g * 6 + 5)
                dve.tensor_tensor(xs, xs, big, ALU.add).then_inc(f_step, 1)
                dve.wait_ge(f_step, g * 6 + 6)
                dve.tensor_tensor(xq, xs, big, ALU.subtract).then_inc(xq_ready, 1)

            def ffn_out(g):
                for t in range(TPC):
                    dve.wait_ge(xq_turned, g * TPC + t + 1)
                    dve.tensor_copy(xqT[:, :, :].rearrange("p k s -> p (k s)"), ffn_tp).then_inc(xqT_ready, 1)
                    dve.wait_ge(ffn_ready, g * TPC + t + 1)
                    if t == 0:
                        dve.wait_ge(y_stored, g * 16 + 16)
                    dve.scalar_tensor_tensor(y_out[:, t, :], ffn_ps, sw,
                                             resid[:, bass.ds(g * TPC + t, 1), :].rearrange("p a d -> p (a d)"),
                                             ALU.mult, ALU.add).then_inc(y_ready, 1)

            with dve.Fori(0, HEADS // 2) as hp:
                for par in range(2):
                    add_head(2 * hp + par, par, 0, 2 * hp + par)
            round_to_float8(0)
            with dve.Fori(1, NG) as g:
                add_head(g * HEADS, 0, g, 0)
                ffn_out(g - 1)
                add_head(g * HEADS + 1, 1, g, 1)
                with dve.Fori(1, HEADS // 2) as hp:
                    for par in range(2):
                        add_head(g * HEADS + 2 * hp + par, par, g, 2 * hp + par)
                round_to_float8(g)
            ffn_out(NG - 1)


def kernel(L0_attn_x, L0_attn_Wq, L0_attn_Wk, L0_attn_Wv, L0_attn_memory, L0_attn_memory_norm, L0_attn_memory_weight,
           L0_ffn_weight, L0_ffn_weight_scale, L0_ffn_input_scale):
    import concourse.bacc as bacc
    from concourse.bass_utils import run_bass_kernel_spmd

    nc = bacc.Bacc("TRN2", target_bir_lowering=False, num_devices=1)
    inputs = {
        "x": np.ascontiguousarray(L0_attn_x).reshape(BATCH * SEQ, DM),
        "Wq": np.ascontiguousarray(L0_attn_Wq),
        "Wk": np.ascontiguousarray(L0_attn_Wk),
        "Wv": np.ascontiguousarray(L0_attn_Wv),
        "memory": np.ascontiguousarray(L0_attn_memory),
        "memory_norm": np.ascontiguousarray(L0_attn_memory_norm),
        "memory_weight": np.ascontiguousarray(L0_attn_memory_weight),
        "weight": np.ascontiguousarray(L0_ffn_weight),
        "weight_scale": np.ascontiguousarray(L0_ffn_weight_scale).reshape(1),
        "input_scale": np.ascontiguousarray(L0_ffn_input_scale).reshape(1),
    }
    aps = [nc.dram_tensor(f"in_{name}", a.shape, mybir.dt.from_np(a.dtype), kind="ExternalInput").ap()
           for name, a in inputs.items()]
    out = nc.dram_tensor("out", (BATCH * SEQ, DM), F32, kind="ExternalOutput").ap()
    q_aug = nc.dram_tensor("q_aug", (NG * HEADS, ROWS, QG * CH), BF16, kind="Internal").ap()
    k_aug = nc.dram_tensor("k_aug", (NG * HEADS, ROWS, CH), BF16, kind="Internal").ap()
    v_aug = nc.dram_tensor("v_aug", (NG, HEADS, P, TPC * VW), F32, kind="Internal").ap()
    guard = nc.dram_tensor("guard", (NG * HEADS, SPLIT, QG * CH), BF16, kind="Internal").ap()
    attention_ffn(nc, *aps, out, q_aug, k_aug, v_aug, guard)
    r = run_bass_kernel_spmd(nc, [{f"in_{name}": a for name, a in inputs.items()}], core_ids=[0])
    return r.results[0]["out"].reshape(BATCH, SEQ, DM)
```

```python
from contextlib import ExitStack

import concourse.bass as bass
import numpy as np
from concourse import mybir
from concourse.alu_op_type import AluOpType as ALU

F32 = mybir.dt.float32
BF16 = mybir.dt.bfloat16
I32 = mybir.dt.int32
U8 = mybir.dt.uint8
ACT = mybir.ActivationFunctionType
AX = mybir.AxisListType
MAX_OVER_PARTITIONS = bass.bass_isa.ReduceOp.max

P = 128
BATCH, SEQ, DM = 2, 2048, 512
HEADS, QG, DH = 8, 4, 16
KV = HEADS * DH
CH = 512
CPB = SEQ // CH
NG = BATCH * CPB
TPC = CH // P
KT = DM // P
NT = NG * TPC
ST = SEQ // P
VW = 32
SPLIT = 3
Q_PART = (0, 0, 0, 1, 1, 2)
K_PART = (0, 1, 2, 0, 1, 0)
TERMS = len(Q_PART)
ROWS = TERMS * DH
AUG = ROWS + SPLIT
SCALE = DH ** -0.5
LN_EPS = 1e-5
FP8_MAX = 448.0
ONE_FREE, TWO_FREE, THREE_FREE = 1, 2, 3
STRIPS = QG * ST
UNIT = 2
SLOTS = 3
UNIT_STRIPS = [(i, i + 1) for i in range(0, STRIPS - UNIT, UNIT)] + [(STRIPS - 2,), (STRIPS - 1,)]
UNITS = len(UNIT_STRIPS)
PTILES = 4
assert UNITS % SLOTS == 0 and ST % PTILES == 0
GUARD_MARGIN = 1.02
GUARD_LIMIT = 130.0 / (SCALE * GUARD_MARGIN)
GUARD_OFFSET = 3.0 / SCALE
FFN_TURN_AT = 11
FFN_PRODUCT_AT = tuple(range(15, 15 + 3 * KT, 3))
MEMORY_AT = 2
W_TURN_AT = 2 * ST - 4 * KT


def attention_ffn(nc, x, Wq, Wk, Wv, memory, memory_norm, memory_weight, weight, weight_scale, input_scale, out,
                  q_aug, k_aug, v_aug, guard):
    x_tiles = x.rearrange("(t p) d -> p t d", p=P)
    out_tiles = out.rearrange("(t p) d -> p t d", p=P)

    with ExitStack() as ctx:
        def sb(name, shape, dt):
            return ctx.enter_context(nc.sbuf_tensor(name, shape, dt))

        def sem(name):
            return ctx.enter_context(nc.semaphore(name))

        ps = ctx.enter_context(nc.psum_tensor("ps", [P, 8, 512], F32))

        resid = sb("resid", [P, NT, DM], F32)
        ident = sb("ident", [P, P], F32)
        ident_bf = sb("ident_bf", [P, P], BF16)
        head_ones = sb("head_ones", [P, P], BF16)
        minus_half = sb("minus_half", [P, TPC], F32)
        eps = sb("eps", [P, TPC], F32)
        half = sb("half", [P, 2 * BATCH], F32)
        k_sum = sb("k_sum", [P, NG], F32)
        k_total = sb("k_total", [P, BATCH], F32)
        k_mean_sq = sb("k_mean_sq", [P, BATCH], BF16)
        wT_ffn = sb("wT_ffn", [P, KT, DM], BF16)
        scalars = sb("scalars", [P, 10], F32)
        mem_w, e_neg, one_plus, w_mem, w_dot, ws_col, s_col, inv_s, sw = (scalars[:, i:i + 1] for i in range(9))
        s_raw = sb("s_raw", [P, 1], BF16)
        q_st = sb("q_st", [P, 2, QG * CH], BF16)
        k_st = sb("k_st", [P, 2, SEQ], BF16)
        v_st = sb("v_st", [P, 2, ST, VW], F32)
        pool = sb("pool", [P, 8192], F32)
        probs = pool[:, 0:PTILES * QG * CH].rearrange("p (a b) -> p a b", a=PTILES)
        by_token = sb("by_token", [P, QG, TPC, VW], F32)
        rden = sb("rden", [P, QG, TPC], F32)
        head_out = sb("head_out", [P, QG, TPC, DH], F32)
        xnT = pool[:, 0:4096].rearrange("p (a k s) -> p a k s", a=2, k=KT)
        xn = pool[:, 4096:6144].rearrange("p (t d) -> p t d", t=TPC)
        wqT = sb("wqT", [P, KT, DM], F32)
        wkT = sb("wkT", [P, KT, KV], F32)
        wvT = sb("wvT", [P, KT, KV], F32)
        mem_aug = sb("mem_aug", [P, KV + 1], F32)
        parts = sb("parts", [P, QG + 1, SPLIT, CH], BF16)
        sq = sb("sq", [P, 2, CH], BF16)
        v_tiles = sb("v_tiles", [P, 2, HEADS, TPC, VW], F32)
        work = sb("work", [P, 10, CH], F32)
        p32, r32, neg, epos, relu = (work[:, 2 * i:2 * i + 2, :] for i in range(5))
        y_out = sb("y_out", [P, TPC, DM], F32)
        wq_raw = y_out
        sigma = y_out
        wkv_raw = sb("wkv_raw", [P, 2, DM], F32)
        xq = wkv_raw[:, :, :].bitcast(BF16).rearrange("p a (b d) -> p (a b) d", b=2)
        w8 = sb("w8", [P, KT, DM], mybir.dt.float8e4)
        w_val = sb("w_val", [P, KT, DM], BF16)
        xqT = sb("xqT", [P, KT, P], BF16)
        last_xqT = pool[:, 0:TPC * KT * P // 2].bitcast(BF16).rearrange("p (t k s) -> p t k s", t=TPC, k=KT)
        stats = sb("stats", [P, TPC, 6], F32)
        moments = sb("moments", [P, 2, TPC, 2], F32)
        var_eps = sb("var_eps", [P, TPC], F32)
        rstd = sb("rstd", [P, 2, TPC], F32)
        rstd_s = sb("rstd_s", [P, TPC], F32)
        rnorm = sb("rnorm", [P, 2, 2], F32)
        norm2 = sb("norm2", [P, NG, QG + 1], F32)
        bound = sb("bound", [P, 9, BATCH], F32)
        range_all = sb("range_all", [P, BATCH], F32)
        widest = sb("widest", [P, 1], F32)
        guard_rest = sb("guard_rest", [P, BATCH], F32)
        guard_parts = sb("guard_parts", [P, BATCH, SPLIT], F32)
        guard_bf = sb("guard_bf", [P, BATCH, SPLIT], BF16)
        ones_row = sb("ones_row", [P, CH], BF16)
        guard_rows = sb("guard_rows", [P, SPLIT, CH], BF16)
        wide = sb("wide", [P, 1], I32)
        row_max = sb("row_max", [P, QG * TPC], F32)
        gm_space = w_val[:, :, :].rearrange("p k o -> p (k o)")[0:QG * TPC, :]
        gm_rest = gm_space[:, 0:2 * P].bitcast(F32)
        gm_parts = gm_space[:, 2 * P:2 * P + SPLIT * P].rearrange("p (i s) -> p i s", i=SPLIT)

        tp = [ps[:, i, :] for i in (0, 1)]
        pj = [ps[:, i, :] for i in (2, 3)]
        vp = ps[:, 4, :]
        am = ps[:, 5:7, 0:2 * (KV + 1)].rearrange("p a (b c) -> p a b c", b=2)
        n2 = ps[:, 7, :]
        k_norm = (vp[:, 0:1], n2[:, 0:1])
        last_am = ps[:, 7, 0:2 * (KV + 1)].rearrange("p (b c) -> p b c", b=2)
        sc = [ps[:, UNIT * i:UNIT * i + UNIT, :] for i in range(SLOTS)]
        acc = [ps[:, i, :] for i in (6, 7)]
        ffn_ps = acc[0]
        ffn_tp = acc[0][:, 0:CH // 2].bitcast(BF16)
        last_ffn_tp = [ps[:, i, 0:CH // 2].bitcast(BF16) for i in range(2)]
        last_ffn = [ps[:, 2 + t, :] for t in range(TPC)]

        x_loaded = [sem(f"x_loaded{i}") for i in range(2)]
        wq_loaded = sem("wq_loaded")
        wkv_loaded = sem("wkv_loaded")
        small_loaded = sem("small_loaded")
        w8_loaded = sem("w8_loaded")
        zeros_set = sem("zeros_set")
        consts_set = sem("consts_set")
        ones_set = sem("ones_set")
        e_neg_ready = sem("e_neg_ready")
        scal = sem("scal")
        w_turned = sem("w_turned")
        w_copied = sem("w_copied")
        dec = sem("dec")
        wf_turned = sem("wf_turned")
        wf_copied = sem("wf_copied")
        stats_ready = sem("stats_ready")
        moments_ready = sem("moments_ready")
        eps_added = sem("eps_added")
        rstd_ready = sem("rstd_ready")
        xn_ready = sem("xn_ready")
        tp_ready = sem("tp_ready")
        xnT_ready = sem("xnT_ready")
        proj_ready = sem("proj_ready")
        p32_ready = sem("p32_ready")
        part1_ready = sem("part1_ready")
        rest_ready = sem("rest_ready")
        part2_ready = sem("part2_ready")
        part3_ready = sem("part3_ready")
        parts_stored = [sem(f"parts_stored{i}") for i in range(QG + 1)]
        pj_read = sem("pj_read")
        epos_ready = sem("epos_ready")
        sigma_ready = sem("sigma_ready")
        sq_ready = sem("sq_ready")
        n2_ready = sem("n2_ready")
        v_proj_ready = sem("v_proj_ready")
        v_tile_ready = sem("v_tile_ready")
        v_stored = [sem(f"v_stored{i}") for i in range(2)]
        am_ready = sem("am_ready")
        am_used = sem("am_used")
        n2_used = sem("n2_used")
        rnorm_ready = sem("rnorm_ready")
        gd = sem("gd")
        bound_in = sem("bound_in")
        k_mean_ready = sem("k_mean_ready")
        k_mean_norm = sem("k_mean_norm")
        bound_root = sem("bound_root")
        range_ready = sem("range_ready")
        bound_all = sem("bound_all")
        guard_rows_ready = sem("guard_rows_ready")
        wide_ready = sem("wide_ready")
        guard_stored = sem("guard_stored")
        gm_loaded = sem("gm_loaded")
        gm_scores = sem("gm_scores")
        gm_scores_used = sem("gm_scores_used")
        gm_turned = sem("gm_turned")
        gm_step = sem("gm_step")
        gm_split = sem("gm_split")
        gm_stored = sem("gm_stored")
        operands_loaded = [sem(f"operands_loaded{i}") for i in range(2)]
        scores_ready = sem("scores_ready")
        probs_ready = sem("probs_ready")
        pv_done = sem("pv_done")
        acc_read = sem("acc_read")
        rden_ready = sem("rden_ready")
        head_out_ready = sem("head_out_ready")
        f_moments = sem("f_moments")
        f_eps = sem("f_eps")
        f_rstd = sem("f_rstd")
        f_step = sem("f_step")
        last_step = sem("last_step")
        xq_ready = sem("xq_ready")
        xq_turned = sem("xq_turned")
        xqT_ready = sem("xqT_ready")
        ffn_ready = sem("ffn_ready")
        y_ready = sem("y_ready")
        y_stored = sem("y_stored")

        block = ctx.enter_context(nc.Block())

        @block.sync
        def _(sp):
            def load_x(c, par):
                sp.dma_start(resid[:, bass.ds(c * TPC, TPC), :], x_tiles[:, bass.ds(c * TPC, TPC), :])\
                    .then_inc(x_loaded[par], 16)

            for o in range(QG + 1):
                sp.sem_inc(parts_stored[o], 16 * TERMS)
            for par in range(2):
                sp.sem_inc(v_stored[par], 16)
            sp.sem_inc(y_stored, 16)
            sp.sem_inc(gm_stored, 16)

            sp.wait_ge(wkv_loaded, 32)
            load_x(1, 1)
            sp.dma_start(w8[:, :, :], weight.rearrange("(a p) i -> p a i", p=P)).then_inc(w8_loaded, 16)

            def store_parts(c, it, last):
                for par in range(2):
                    if not last:
                        sp.wait_ge(x_loaded[par], 16 * it + 16)
                        load_x(c + par + 2, par)
                    for o in range(QG + 1):
                        sp.wait_ge(part3_ready, (c + par) * (QG + 1) + o + 1)
                        if last and par == 1:
                            prefetch(o)
                        for r in range(TERMS):
                            rows = slice(r * DH, r * DH + DH)
                            if o < QG:
                                dst = q_aug[bass.ds((c + par) * HEADS, HEADS), rows, o * CH:o * CH + CH]
                                src = parts[:, o, Q_PART[r], :]
                            else:
                                dst = k_aug[bass.ds((c + par) * HEADS, HEADS), rows, :]
                                src = parts[:, o, K_PART[r], :]
                            sp.dma_start(dst, src).then_inc(parts_stored[o], 16)
                    sp.wait_ge(v_tile_ready, c + par + 1 + ONE_FREE)
                    sp.dma_start(v_dst(c + par), v_tiles[:, par, :, :, :].rearrange("p h t w -> p h (t w)"))\
                        .then_inc(v_stored[par], 16)
                    if last and par == 0:
                        store_guard(0)

            def store_guard(b):
                sp.wait_ge(guard_rows_ready, (b + 1) * SPLIT)
                for c in range(b * CPB, (b + 1) * CPB):
                    for i in range(SPLIT):
                        sp.dma_start(guard[c * HEADS:(c + 1) * HEADS, i, :].rearrange("h (o s) -> h o s", o=QG),
                                     guard_rows[0:P:DH, i, :].unsqueeze(1).to_broadcast([HEADS, QG, CH]))\
                            .then_inc(guard_stored, 16)

            def prefetch(o):
                if o < 2:
                    load_qk(o, 0, o, o, operands_loaded[o])
                elif o == 2:
                    sp.wait_ge(guard_stored, 16 * CPB * SPLIT)
                    for h in range(2):
                        load_guard(h, h, operands_loaded[h])
                elif o == 3:
                    for h in range(2):
                        load_v(0, h, h)

            def v_dst(c):
                return v_aug[bass.ds(c, 1), :, :, :].rearrange("a h p w -> p (a h) w")

            def load_qk(n, g, h, par, done):
                sp.dma_start(q_st[0:ROWS, par, :], q_aug[bass.ds(n, 1), :, :].rearrange("a r s -> (a r) s"))\
                    .then_inc(done, 16)
                b4 = (g // CPB) * CPB
                sp.dma_start(k_st[0:ROWS, par, :].rearrange("r (c s) -> r c s", c=CPB), k_src(b4, h)).then_inc(done, 16)

            def k_src(b4, h):
                return k_aug[bass.ds(b4 * HEADS, CPB * HEADS), :, :]\
                    .rearrange("(c h) r s -> h r c s", c=CPB)[h, :, :, :]

            def load_v(g, h, par):
                sp.dma_start(v_st[:, par, :, :].rearrange("p (c t) w -> p c (t w)", c=CPB), v_src((g // CPB) * CPB, h))\
                    .then_inc(operands_loaded[par], 16)

            def v_src(b4, h):
                return v_aug[bass.ds(b4, CPB), h, :, :].rearrange("c p w -> p c w")

            def load_guard(n, par, done):
                sp.dma_start(q_st[ROWS:AUG, par, :], guard[bass.ds(n, 1), :, :].rearrange("a i s -> (a i) s"))\
                    .then_inc(done, 16)

            with sp.Fori(0, NG // 2 - 1) as it:
                store_parts(2 * it, it, False)
            store_parts(NG - 2, NG // 2 - 1, True)

            store_guard(1)
            for o in range(QG + 1):
                sp.wait_ge(parts_stored[o], 16 * TERMS * (NG + 1))
            for par in range(2):
                sp.wait_ge(v_stored[par], 16 * (NG // 2 + 1))
            sp.wait_ge(guard_stored, 16 * NG * SPLIT)

            sp.wait_ge(wide_ready, 1)
            bound_too_wide = sp.value_load(wide[0:1, 0:1], min_val=0, max_val=1)
            with sp.If(bound_too_wide):
                for par in range(2):
                    sp.wait_ge(operands_loaded[par], 64)
                with sp.Fori(0, NG) as g:
                    for h in range(HEADS):
                        n = g * HEADS + h
                        sp.wait_ge(gm_stored, 16 * n + 16)
                        load_qk(n, g, h, 0, gm_loaded)
                        sp.wait_ge(gm_split, n + 1)
                        sp.dma_start(guard[bass.ds(n, 1), :, :].rearrange("a i (u p) -> u (a i) p", p=P),
                                     gm_parts[:, :, :]).then_inc(gm_stored, 16)
                sp.wait_ge(gm_stored, 16 * (NG * HEADS + 1))
                load_qk(0, 0, 0, 0, gm_loaded)
                for h in range(2):
                    load_guard(h, h, gm_loaded)
                sp.wait_ge(gm_loaded, 32 * (NG * HEADS + 2))

            def load_block(g, h):
                n = g * HEADS + h
                par = h % 2
                sp.wait_ge(pv_done, (n - 1) * ST)
                load_qk(n, g, h, par, operands_loaded[par])
                load_v(g, h, par)
                load_guard(n, par, operands_loaded[par])

            for h in range(2, HEADS):
                load_block(0, h)
            def store_chunk(g):
                sp.wait_ge(y_ready, (g + 1) * TPC + ONE_FREE)
                sp.dma_start(out_tiles[:, bass.ds(g * TPC, TPC), :], y_out[:, :, :]).then_inc(y_stored, 16)

            for h in range(HEADS):
                load_block(1, h)
            with sp.Fori(2, NG) as g:
                for h in range(HEADS):
                    if h == 2:
                        store_chunk(g - 2)
                    load_block(g, h)
            store_chunk(NG - 2)
            for t in range(TPC):
                sp.wait_ge(y_ready, (NG - 1) * TPC + t + 1 + ONE_FREE)
                sp.dma_start(out_tiles[:, NT - TPC + t, :], y_out[:, t, :]).then_inc(y_stored, 16)
            sp.wait_ge(y_stored, 16 * (NG + TPC))

        @block.gpsimd
        def _(pool_e):
            pool_e.memset(ident[:, :], 0.0).then_inc(zeros_set, 1)
            pool_e.memset(ident_bf[:, :], 0.0).then_inc(zeros_set, 1)
            pool_e.memset(head_ones[:, :], 1.0).then_inc(zeros_set, 1)
            pool_e.wait_ge(zeros_set, 3)
            for m in (ident, ident_bf):
                pool_e.affine_select(out=m[:, :], in_=m[:, :], compare_op=ALU.not_equal, fill=1.0, base=0,
                                     pattern=[[-1, P]], channel_multiplier=1).then_inc(consts_set, 1)
            blocks = head_ones[:, :].rearrange("p (a b) -> p a b", b=DH)
            pool_e.affine_select(out=blocks, in_=blocks, compare_op=ALU.is_ge, fill=0.0, base=0,
                                 pattern=[[-DH, HEADS], [0, DH]], channel_multiplier=1).then_inc(zeros_set, 1)
            pool_e.wait_ge(zeros_set, 4)
            pool_e.affine_select(out=blocks, in_=blocks, compare_op=ALU.is_ge, fill=0.0, base=DH - 1,
                                 pattern=[[DH, HEADS], [0, DH]], channel_multiplier=-1).then_inc(consts_set, 1)
            pool_e.memset(minus_half[:, :], -0.5).then_inc(consts_set, 1)
            pool_e.memset(half[:, :], 0.5).then_inc(consts_set, 1)
            pool_e.memset(eps[:, :], LN_EPS).then_inc(consts_set, 1)
            pool_e.memset(v_tiles[:, :, :, :, DH:VW], 0.0).then_inc(zeros_set, 1)
            pool_e.wait_ge(zeros_set, 5)
            pool_e.memset(v_tiles[:, :, :, :, DH:DH + 1], 1.0).then_inc(ones_set, 1)
            pool_e.memset(ones_row[:, :], 1.0).then_inc(ones_set, 1)
            pool_e.wait_ge(ones_set, 2)
            pool_e.memset(k_st[ROWS:P, :, :], 1.0).then_inc(ones_set, 1)
            pool_e.wait_ge(consts_set, 6)
            pool_e.wait_ge(ones_set, 3)

            def rstd_of(c, par):
                pool_e.wait_ge(moments_ready, c + 1)
                pool_e.tensor_tensor(var_eps[:, :], moments[:, par, :, 1], eps[:, :], ALU.add)\
                    .then_inc(eps_added, 1)
                pool_e.wait_ge(eps_added, c + 1)
                pool_e.tensor_tensor(rstd[:, par, :], var_eps[:, :], minus_half[:, :], ALU.pow).then_inc(rstd_ready, 1)

            def bound_roots(b):
                pool_e.wait_ge(bound_in, 2 * b + 2)
                pool_e.tensor_tensor(bound[:, 4:6, b:b + 1], bound[:, 2:4, b:b + 1], half[:, 0:2].unsqueeze(2), ALU.pow)\
                    .then_inc(bound_root, 1)

            def chunk(c, par, last, first_guard=False):
                for o in range(QG + 1):
                    if o == 2 and not last:
                        pool_e.wait_ge(sq_ready, c * (QG + 1) + o)
                        rstd_of(c + 1, 1 - par)
                        pool_e.wait_ge(rstd_ready, c + 2)
                    i = c * (QG + 1) + o
                    slot = (par * (QG + 1) + o) % 2
                    if o == 3 and first_guard:
                        pool_e.wait_ge(sq_ready, i)
                        bound_roots(0)
                        pool_e.wait_ge(bound_root, 1)
                    pool_e.wait_ge(part1_ready, i + 1)
                    pool_e.wait_ge(n2_ready, i)
                    pool_e.tensor_tensor(sq[:, slot, :], parts[:, o, 0, :], parts[:, o, 0, :], ALU.mult)\
                        .then_inc(sq_ready, 1)

            rstd_of(0, 0)
            pool_e.wait_ge(rstd_ready, 1)
            chunk(0, 0, False)
            chunk(1, 1, False)
            with pool_e.Fori(1, NG // 2 - 1) as it:
                chunk(2 * it, 0, False)
                chunk(2 * it + 1, 1, False)
            chunk(NG - 2, 0, False, first_guard=True)
            chunk(NG - 1, 1, True)

            pool_e.wait_ge(sq_ready, NG * (QG + 1))
            bound_roots(1)
            pool_e.wait_ge(range_ready, 2)
            pool_e.partition_all_reduce(range_all[:, :], bound[:, 6, :], P, MAX_OVER_PARTITIONS).then_inc(bound_all, 1)
            pool_e.wait_ge(bound_all, 1)

            with pool_e.Fori(0, NG) as g:
                pool_e.wait_ge(f_moments, g + 1)
                pool_e.tensor_tensor(var_eps[:, :], moments[:, 0, :, 1], eps[:, :], ALU.add).then_inc(f_eps, 1)
                pool_e.wait_ge(f_eps, g + 1)
                pool_e.tensor_tensor(rstd[:, 0, :], var_eps[:, :], minus_half[:, :], ALU.pow).then_inc(f_rstd, 1)
                pool_e.wait_ge(f_rstd, g + 1)

        @block.scalar
        def _(act):
            act.dma_start(resid[:, 0:TPC, :], x_tiles[:, 0:TPC, :]).then_inc(x_loaded[0], 16)
            act.dma_start(wq_raw[:, :, :], Wq.rearrange("(a p) i -> p a i", p=P)).then_inc(wq_loaded, 16)
            act.dma_start(wkv_raw[:, 0, :], Wk).then_inc(wkv_loaded, 16)
            act.dma_start(wkv_raw[:, 1, :], Wv).then_inc(wkv_loaded, 16)
            act.dma_start(mem_w, memory_weight.partition_broadcast(P)).then_inc(small_loaded, 16)
            act.dma_start(ws_col, weight_scale.partition_broadcast(P)).then_inc(small_loaded, 16)
            act.dma_start(s_raw[:, :], input_scale.partition_broadcast(P)).then_inc(small_loaded, 16)
            act.dma_start(mem_aug[:, 0:KV], memory).then_inc(small_loaded, 16)
            act.dma_start(mem_aug[:, KV:KV + 1], memory_norm).then_inc(small_loaded, 16)
            act.sem_inc(xnT_ready, TWO_FREE)
            act.sem_inc(p32_ready, TWO_FREE)
            act.sem_inc(pj_read, ONE_FREE)
            act.sem_inc(v_tile_ready, ONE_FREE)
            act.sem_inc(probs_ready, THREE_FREE)
            act.wait_ge(small_loaded, 80)
            act.activation(e_neg, mem_w, ACT.Exp, scale=-1.0).then_inc(e_neg_ready, 1)
            for j in range(KT + 2):
                act.wait_ge(w_turned, j + 1)
                if j < KT:
                    dst = wqT[:, j, :]
                else:
                    dst = (wkT, wvT)[j - KT][:, :, :].rearrange("p k o -> p (k o)")
                src = ps[:, j, :]
                act.activation(dst, src, ACT.Copy).then_inc(w_copied, 1)

            def copy_xnT(c, par, ks, first=False):
                if not first:
                    act.wait_ge(v_proj_ready, c)
                for k in ks:
                    act.wait_ge(tp_ready, c * KT + k + 1)
                    act.activation(xnT[:, par, k, :], tp[k % 2], ACT.Copy).then_inc(xnT_ready, 1)

            def exp_neg(c, par, o):
                act.wait_ge(pj_read, c * QG + o + 1 + ONE_FREE)
                act.activation(epos[:, o % 2, :], neg[:, o % 2, :], ACT.Exp, scale=-1.0).then_inc(epos_ready, 1)

            def second_part(c, par, o):
                act.wait_ge(rest_ready, c * (QG + 1) + o + 1 + TWO_FREE)
                act.activation(parts[:, o, 1, :], r32[:, (par * (QG + 1) + o) % 2, :], ACT.Copy).then_inc(part2_ready, 1)

            def chunk(c, par, last):
                for o in range(QG + 1):
                    i = c * (QG + 1) + o
                    slot = (par * (QG + 1) + o) % 2
                    act.wait_ge(proj_ready, i + 1)
                    act.wait_ge(rest_ready, i + 1)
                    act.activation(p32[:, slot, :], pj[slot], ACT.Copy).then_inc(p32_ready, 1)
                    if o < QG:
                        act.wait_ge(sigma_ready, c * QG + o + 1)
                        act.activation(relu[:, o % 2, :], pj[slot], ACT.Relu)
                        act.activation(neg[:, o % 2, :], pj[slot], ACT.Relu, scale=-1.0).then_inc(pj_read, 1)
                    if o < QG:
                        exp_neg(c, par, o)
                        second_part(c, par, o)
                if not last:
                    copy_xnT(c + 1, 1 - par, range(KT // 2))
                second_part(c, par, QG)
                act.wait_ge(v_proj_ready, c + 1 + ONE_FREE)
                act.wait_ge(v_stored[par], (c - par) * 8 + 16)
                act.wait_ge(scal, 4)
                act.activation(v_tiles[:, par, :, :, 0:DH], vp.rearrange("p (t h d) -> p h t d", t=TPC, h=HEADS),
                               ACT.Copy, scale=w_dot).then_inc(v_tile_ready, 1)
                if not last:
                    copy_xnT(c + 1, 1 - par, range(KT // 2, KT))

            copy_xnT(0, 0, range(KT), first=True)
            with act.Fori(0, NG // 2 - 1) as it:
                chunk(2 * it, 0, False)
                chunk(2 * it + 1, 1, False)
            chunk(NG - 2, 0, False)
            chunk(NG - 1, 1, True)
            with act.Fori(0, NG * HEADS // 2) as pair:
                for v in range(2 * UNITS):
                    strips = UNIT_STRIPS[v % UNITS]
                    j, q = divmod(strips[0], QG)
                    act.wait_ge(scores_ready, pair * (2 * UNITS) + v + 1)
                    act.activation(probs[:, j % PTILES, q * CH:(q + len(strips)) * CH],
                                   sc[v % SLOTS][:, 0:len(strips), :].rearrange("p a b -> p (a b)"), ACT.Exp,
                                   scale=SCALE).then_inc(probs_ready, 1)
            for t in range(TPC):
                act.wait_ge(xq_turned, (NG - 1) * TPC + t + 1)
                act.activation(last_xqT[:, t, :, :].rearrange("p k s -> p (k s)"), last_ffn_tp[t % 2], ACT.Copy)\
                    .then_inc(xqT_ready, 1)

        @block.tensor
        def _(pe):
            pe.sem_inc(v_proj_ready, ONE_FREE)
            pe.wait_ge(consts_set, 6)
            pe.wait_ge(wq_loaded, 16)
            for j in range(KT + 2):
                if j == KT:
                    pe.wait_ge(wkv_loaded, 32)
                for a in range(KT):
                    src = wq_raw[:, a, j * P:j * P + P] if j < KT else wkv_raw[:, j - KT, a * P:a * P + P]
                    last = pe.transpose(ps[:, j, a * P:a * P + P], src, ident[:, :])
                last.then_inc(w_turned, 1)
            def turn_xn(c, ks):
                pe.wait_ge(xn_ready, c + 1)
                for k in ks:
                    pe.wait_ge(xnT_ready, c * KT + k + 1)
                    for t in range(TPC):
                        last = pe.transpose(tp[k % 2][:, t * P:t * P + P], xn[:, t, k * P:k * P + P], ident[:, :])
                    last.then_inc(tp_ready, 1)

            def norms(c, par, o):
                i = c * (QG + 1) + o
                pe.wait_ge(sq_ready, i + 1)
                pe.wait_ge(n2_used, i + 1)
                pe.matmul(n2, head_ones[:, :], sq[:, (par * (QG + 1) + o) % 2, :], start=True, stop=True)\
                    .then_inc(n2_ready, 1)

            def memory_products(c, q):
                pe.wait_ge(sigma_ready, c * QG + q + 1 + TWO_FREE)
                pe.wait_ge(am_used, c * QG + q + ONE_FREE)
                for t in range(TPC):
                    last = pe.matmul(am[:, t // 2, t % 2, :], sigma[:, q, t * P:t * P + P], mem_aug[:, :],
                                     start=True, stop=True)
                last.then_inc(am_ready, 1)

            def mean_key_norm(b):
                pe.wait_ge(k_mean_ready, b + 1)
                pe.matmul(k_norm[b], head_ones[:, :], k_mean_sq[:, b:b + 1], start=True, stop=True).then_inc(k_mean_norm, 1)

            def chunk(c, par, first_chunk=False, first_guard=False, last_chunk=False):
                for o in range(QG + 1):
                    if o == 1:
                        pe.wait_ge(p32_ready, c * (QG + 1) + TWO_FREE)
                    else:
                        pe.wait_ge(pj_read, c * QG + max(o - 1, 0) + ONE_FREE)
                    for k in range(KT):
                        if o == 0:
                            pe.wait_ge(xnT_ready, c * KT + k + 1 + TWO_FREE)
                        w = wqT[:, k, o * P:o * P + P] if o < QG else wkT[:, k, :]
                        last = pe.matmul(pj[(par * (QG + 1) + o) % 2], w, xnT[:, par, k, :],
                                         start=(k == 0), stop=(k == KT - 1))
                    last.then_inc(proj_ready, 1)
                    if o >= 1:
                        norms(c, par, o - 1)
                    if first_guard and o == 1:
                        pe.wait_ge(v_tile_ready, c + 1)
                        mean_key_norm(0)
                    if not first_chunk and o < QG:
                        memory_products(c - 1, o)
                if not last_chunk:
                    turn_xn(c + 1, range(KT // 2))
                pe.wait_ge(v_tile_ready, c + 1)
                if first_guard:
                    pe.wait_ge(bound_in, 2)
                for t in range(TPC):
                    for k in range(KT):
                        last = pe.matmul(vp[:, t * P:t * P + P], xnT[:, par, k, t * P:t * P + P], wvT[:, k, :],
                                         start=(k == 0), stop=(k == KT - 1))
                last.then_inc(v_proj_ready, 1)
                norms(c, par, QG)
                if not last_chunk:
                    turn_xn(c + 1, range(KT // 2, KT))

            pe.wait_ge(w_copied, 2)
            turn_xn(0, range(KT))
            pe.wait_ge(w_copied, KT + 2)
            pe.wait_ge(scal, 4)
            chunk(0, 0, first_chunk=True)
            chunk(1, 1)
            with pe.Fori(1, NG // 2 - 1) as it:
                chunk(2 * it, 0)
                chunk(2 * it + 1, 1)
            chunk(NG - 2, 0, first_guard=True)
            chunk(NG - 1, 1, last_chunk=True)
            mean_key_norm(1)
            pe.wait_ge(am_used, (NG - 1) * QG + ONE_FREE)
            pe.wait_ge(v_tile_ready, NG + ONE_FREE)

            pe.wait_ge(wide_ready, 1)
            bound_too_wide = pe.value_load(wide[0:1, 0:1], min_val=0, max_val=1)
            with pe.If(bound_too_wide):
                with pe.Fori(0, NG * HEADS) as n:
                    pe.wait_ge(gm_loaded, n * 32 + 32)
                    for u in range(QG * TPC):
                        pe.wait_ge(gm_scores_used, n * (QG * TPC) + u + ONE_FREE)
                        for c4 in range(CPB):
                            last = pe.matmul(ps[:, c4, :], q_st[0:ROWS, 0, u * P:u * P + P],
                                             k_st[0:ROWS, 0, c4 * CH:c4 * CH + CH], start=True, stop=True)
                        last.then_inc(gm_scores, 1)
                    pe.wait_ge(gm_scores_used, n * (QG * TPC) + QG * TPC + ONE_FREE)
                    pe.transpose(ps[0:QG * TPC, 6, 0:P], row_max[:, :], ident[:, :]).then_inc(gm_turned, 1)
                pe.wait_ge(gm_loaded, 32 * (NG * HEADS + 2))

            def scores(n, par, u):
                pe.wait_ge(probs_ready, n * UNITS + u - SLOTS + 1 + THREE_FREE)
                for x, strip in enumerate(UNIT_STRIPS[u]):
                    j, q = divmod(strip, QG)
                    last = pe.matmul(sc[u % SLOTS][:, x, :], k_st[0:AUG, par, j * P:j * P + P],
                                     q_st[0:AUG, par, q * CH:q * CH + CH], start=True, stop=True)
                last.then_inc(scores_ready, 1)

            def weigh_v(n, par, u):
                j, q = divmod(UNIT_STRIPS[u][-1], QG)
                if q == QG - 1:
                    by_place = probs[:, j % PTILES, :].rearrange("p (i c s) -> p c i s", c=P // VW, s=VW)
                    for c in range(P // VW):
                        last = pe.matmul(acc[par][VW * c:VW * c + VW, :].rearrange("v (i s) -> v i s", s=VW),
                                         v_st[:, par, j, :], by_place[:, c, :, :], start=(j == 0), stop=(j == ST - 1))
                    last.then_inc(pv_done, 1)

            def ffn_turn(g, t):
                pe.wait_ge(xq_ready, g + 1)
                pe.wait_ge(y_ready, g * TPC + t + ONE_FREE)
                for k in range(KT):
                    last = pe.transpose(ffn_tp[:, k * P:k * P + P],
                                        xq[:, bass.ds(t, 1), k * P:k * P + P].rearrange("p a d -> p (a d)"), ident_bf[:, :])
                last.then_inc(xq_turned, 1)

            def ffn_product(g, t, k):
                if k == 0:
                    pe.wait_ge(xqT_ready, g * TPC + t + 1)
                last = pe.matmul(ffn_ps, xqT[:, k, :], wT_ffn[:, k, :], start=(k == 0), stop=(k == KT - 1))
                if k == KT - 1:
                    last.then_inc(ffn_ready, 1)

            def last_memory_products(i):
                q, half_q = divmod(i, 2)
                pe.wait_ge(sigma_ready, NG * QG + TWO_FREE)
                pe.wait_ge(am_used, (NG - 1) * QG + i + ONE_FREE)
                for t in range(2):
                    tokens = (2 * half_q + t) * P
                    last = pe.matmul(last_am[:, t, :], sigma[:, q, tokens:tokens + P], mem_aug[:, :], start=True, stop=True)
                last.then_inc(am_ready, 1)

            def turn_ffn_weight(k):
                if k == 0:
                    pe.wait_ge(dec, 8)
                    pe.wait_ge(acc_read, 1 + TWO_FREE)
                pe.wait_ge(wf_copied, k)
                for a in range(KT):
                    last = pe.transpose(ffn_tp[:, a * P:a * P + P], w_val[:, a, k * P:k * P + P], ident_bf[:, :])
                last.then_inc(wf_turned, 1)

            def pair(n0, trip, first=False, weight_read=False, ffn=None):
                for par in range(2):
                    n = n0 + par
                    pe.wait_ge(operands_loaded[par], trip * 64 + 64)
                    for u in range(UNITS):
                        scores(n, par, u)
                        if u >= SLOTS:
                            if u == SLOTS:
                                pe.wait_ge(acc_read, n + 1)
                                if first and par == 1:
                                    pe.wait_ge(am_used, (NG + 1) * QG + ONE_FREE)
                                if weight_read and par == 0:
                                    pe.wait_ge(wf_copied, KT)
                                if ffn is not None and par == 0:
                                    g, t = ffn
                                    pe.wait_ge(y_ready, g * TPC + t + ONE_FREE)
                            weigh_v(n, par, u - SLOTS)
                        elif not (first and par == 0):
                            weigh_v(n - 1, 1 - par, UNITS + u - SLOTS)
                        if first and par == 0:
                            if u % 2 == 0 and 0 <= u - MEMORY_AT < 4 * QG:
                                last_memory_products((u - MEMORY_AT) // 2)
                        if first and par == 1 and u in range(W_TURN_AT, W_TURN_AT + 4 * KT, 4):
                            turn_ffn_weight((u - W_TURN_AT) // 4)
                        if ffn is not None and par == 1:
                            if u == FFN_TURN_AT:
                                pe.wait_ge(acc_read, n + TWO_FREE)
                                ffn_turn(*ffn)
                            if u in FFN_PRODUCT_AT:
                                ffn_product(*ffn, FFN_PRODUCT_AT.index(u))

            pairs = HEADS // 2
            pair(0, 0, first=True)
            with pe.Fori(1, pairs) as hp:
                pair(2 * hp, hp, weight_read=True)
            with pe.Fori(1, NG) as g:
                with pe.Fori(0, pairs) as hp:
                    pair(g * HEADS + 2 * hp, g * pairs + hp, ffn=(g - 1, hp))
            last_n = NG * HEADS - 1
            for u in range(UNITS - SLOTS, UNITS):
                pe.wait_ge(probs_ready, last_n * UNITS + u + 1 + THREE_FREE)
                weigh_v(last_n, 1, u)

            def last_ffn_turn(t):
                pe.wait_ge(xq_ready, NG + t)
                if t >= 2:
                    pe.wait_ge(xqT_ready, (NG - 1) * TPC + t - 1)
                for k in range(KT):
                    last = pe.transpose(last_ffn_tp[t % 2][:, k * P:k * P + P], xq[:, t, k * P:k * P + P], ident_bf[:, :])
                last.then_inc(xq_turned, 1)

            def last_ffn_product(t):
                pe.wait_ge(xqT_ready, (NG - 1) * TPC + t + 1)
                for k in range(KT):
                    last = pe.matmul(last_ffn[t], last_xqT[:, t, k, :], wT_ffn[:, k, :], start=(k == 0), stop=(k == KT - 1))
                last.then_inc(ffn_ready, 1)

            for t in range(0, TPC, 2):
                last_ffn_turn(t)
                last_ffn_turn(t + 1)
                last_ffn_product(t)
                last_ffn_product(t + 1)

        @block.vector
        def _(dve):
            dve.sem_inc(rest_ready, TWO_FREE)
            dve.sem_inc(sigma_ready, TWO_FREE)
            dve.sem_inc(am_used, ONE_FREE)
            dve.sem_inc(acc_read, TWO_FREE)
            dve.sem_inc(n2_used, ONE_FREE)
            dve.sem_inc(gm_scores_used, ONE_FREE)
            dve.sem_inc(y_ready, ONE_FREE)

            def statistics(c):
                for t in range(TPC):
                    last = dve.bn_stats(stats[:, t, :], resid[:, bass.ds(c * TPC + t, 1), :].rearrange("p a d -> p (a d)"))
                last.then_inc(stats_ready, 1)

            def mean_and_variance(par):
                for t in range(TPC):
                    last = dve.bn_aggr(moments[:, par, t, :], stats[:, t, :])
                last.then_inc(moments_ready, 1)

            def normalise(c, par):
                dve.wait_ge(rstd_ready, c + 1)
                dve.wait_ge(tp_ready, c * KT)
                for t in range(TPC):
                    last = dve.tensor_scalar(xn[:, t, :], resid[:, bass.ds(c * TPC + t, 1), :].rearrange("p a d -> p (a d)"),
                                             moments[:, par, t, 0:1], rstd[:, par, t:t + 1], ALU.subtract, ALU.mult)
                last.then_inc(xn_ready, 1)

            dve.wait_ge(x_loaded[0], 16)
            statistics(0)
            dve.wait_ge(stats_ready, 1)
            mean_and_variance(0)
            normalise(0, 0)
            dve.wait_ge(e_neg_ready, 1)
            dve.tensor_scalar(one_plus, e_neg, 1.0, None, ALU.add).then_inc(scal, 1)
            dve.wait_ge(scal, 1)
            dve.reciprocal(w_mem, one_plus).then_inc(scal, 1)
            dve.wait_ge(scal, 2)
            dve.tensor_scalar(w_dot, w_mem, -1.0, 1.0, ALU.mult, ALU.add).then_inc(scal, 1)
            dve.tensor_scalar(mem_aug[:, 0:KV], mem_aug[:, 0:KV], w_mem, None, ALU.mult).then_inc(scal, 1)
            dve.tensor_copy(s_col, s_raw[:, :]).then_inc(scal, 1)
            dve.wait_ge(scal, 5)
            dve.reciprocal(inv_s, s_col).then_inc(scal, 1)
            dve.tensor_tensor(sw, s_col, ws_col, ALU.mult).then_inc(scal, 1)

            def finish(c, par, o):
                i = c * (QG + 1) + o
                slot = (par * (QG + 1) + o) % 2
                dve.wait_ge(part2_ready, i + 1)
                dve.tensor_tensor(parts[:, o, 2, :], r32[:, slot, :], parts[:, o, 1, :], ALU.subtract)\
                    .then_inc(part3_ready, 1)
                if o < QG:
                    dve.wait_ge(epos_ready, c * QG + o + 1)
                    dve.scalar_tensor_tensor(sigma[:, o, :], epos[:, o % 2, :], -1.0, relu[:, o % 2, :],
                                             ALU.add, ALU.add).then_inc(sigma_ready, 1)
                dve.wait_ge(n2_ready, i + 1)
                dve.tensor_reduce(norm2[:, bass.ds(c, 1), o], n2, AX.X, ALU.max).then_inc(n2_used, 1)

            def memory_part(c, q):
                dve.wait_ge(am_ready, c * QG + q + 1)
                dve.reciprocal(rnorm[:, :, :], am[:, :, :, KV]).then_inc(rnorm_ready, 1)
                dve.wait_ge(rnorm_ready, c * QG + q + 1)
                for t in range(TPC):
                    row = resid[:, bass.ds(c * TPC + t, 1), q * KV:q * KV + KV].rearrange("p a d -> p (a d)")
                    last = dve.scalar_tensor_tensor(row, am[:, t // 2, t % 2, 0:KV], rnorm[:, t // 2, t % 2:t % 2 + 1], row,
                                                    ALU.mult, ALU.add)
                last.then_inc(am_used, 1)

            GUARD_STEPS = 10

            def guard_sums(b):
                dve.wait_ge(n2_used, (b + 1) * CPB * (QG + 1) + ONE_FREE)
                chunks, step = slice(b * CPB, (b + 1) * CPB), b * GUARD_STEPS
                dve.tensor_reduce(k_total[:, b:b + 1], k_sum[:, chunks], AX.X, ALU.add).then_inc(gd, 1)
                dve.tensor_reduce(bound[:, 0, b:b + 1], norm2[:, chunks, 0:QG], AX.XY, ALU.max).then_inc(gd, 1)
                dve.tensor_reduce(bound[:, 1, b:b + 1], norm2[:, chunks, QG], AX.X, ALU.max).then_inc(gd, 1)
                dve.wait_ge(gd, step + 1)
                dve.scalar_tensor_tensor(k_mean_sq[:, b:b + 1], k_total[:, b:b + 1], 1.0 / SEQ ** 2, k_total[:, b:b + 1],
                                         ALU.mult, ALU.mult).then_inc(k_mean_ready, 1)
                dve.wait_ge(gd, step + 3)
                dve.tensor_tensor(bound[:, 2, b:b + 1], bound[:, 0, b:b + 1], bound[:, 1, b:b + 1], ALU.mult).then_inc(bound_in, 1)

            def guard_products(b):
                dve.wait_ge(k_mean_norm, b + 1)
                dve.tensor_tensor(bound[:, 3, b:b + 1], bound[:, 0, b:b + 1], k_norm[b], ALU.mult).then_inc(bound_in, 1)

            def guard_value(b):
                step = b * GUARD_STEPS + 3
                dve.wait_ge(bound_root, b + 1)
                dve.tensor_tensor(bound[:, 6, b:b + 1], bound[:, 4, b:b + 1], bound[:, 5, b:b + 1], ALU.add).then_inc(range_ready, 1)
                dve.tensor_tensor(bound[:, 7, b:b + 1], bound[:, 4, b:b + 1], bound[:, 5, b:b + 1], ALU.subtract).then_inc(gd, 1)
                dve.wait_ge(gd, step + 1)
                dve.tensor_scalar(bound[:, 8, b:b + 1], bound[:, 7, b:b + 1], -GUARD_MARGIN / 2, GUARD_OFFSET, ALU.mult, ALU.add)\
                    .then_inc(gd, 1)
                dve.wait_ge(gd, step + 2)
                dve.tensor_copy(guard_bf[:, b, 0:1], bound[:, 8, b:b + 1]).then_inc(gd, 1)
                dve.wait_ge(gd, step + 3)
                dve.tensor_tensor(guard_rest[:, b:b + 1], bound[:, 8, b:b + 1], guard_bf[:, b, 0:1], ALU.subtract).then_inc(gd, 1)
                dve.wait_ge(gd, step + 4)
                dve.tensor_copy(guard_bf[:, b, 1:2], guard_rest[:, b:b + 1]).then_inc(gd, 1)
                dve.wait_ge(gd, step + 5)
                dve.tensor_tensor(guard_bf[:, b, 2:3], guard_rest[:, b:b + 1], guard_bf[:, b, 1:2], ALU.subtract).then_inc(gd, 1)
                dve.wait_ge(gd, step + 6)
                dve.tensor_copy(guard_parts[:, b, :], guard_bf[:, b, :]).then_inc(gd, 1)

            def fill_guard_rows(b):
                dve.wait_ge(gd, (b + 1) * GUARD_STEPS)
                if b == 0:
                    dve.wait_ge(ones_set, 3)
                else:
                    dve.wait_ge(guard_stored, 16 * CPB * SPLIT)
                for i in range(SPLIT):
                    dve.tensor_scalar(guard_rows[:, i, :], ones_row[:, :], guard_parts[:, b, i:i + 1], None, ALU.mult)\
                        .then_inc(guard_rows_ready, 1)

            def chunk(c, par, first_chunk=False, first_guard=False, last_chunk=False):
                for o in range(QG + 1):
                    i = c * (QG + 1) + o
                    slot = (par * (QG + 1) + o) % 2
                    if o == 1 and not last_chunk:
                        dve.wait_ge(stats_ready, c + 2)
                    dve.wait_ge(p32_ready, i + 1 + TWO_FREE)
                    dve.wait_ge(parts_stored[o], (c + 1) * (16 * TERMS))
                    dve.tensor_copy(parts[:, o, 0, :], p32[:, slot, :]).then_inc(part1_ready, 1)
                    if o == 1 and not last_chunk:
                        mean_and_variance(1 - par)
                    if o == QG:
                        dve.tensor_reduce(k_sum[:, bass.ds(c, 1)], p32[:, slot, :], AX.X, ALU.add)
                    dve.wait_ge(part1_ready, i + 1)
                    dve.tensor_tensor(r32[:, slot, :], p32[:, slot, :], parts[:, o, 0, :], ALU.subtract)\
                        .then_inc(rest_ready, 1)
                    if o >= 1:
                        finish(c, par, o - 1)
                    if not first_chunk and o < QG:
                        memory_part(c - 1, o)
                    if first_guard:
                        if o == 0:
                            guard_sums(0)
                        elif o == 1:
                            guard_products(0)
                        elif o == 3:
                            guard_value(0)
                            fill_guard_rows(0)
                    if o == 2 and not last_chunk:
                        normalise(c + 1, 1 - par)
                if not (first_guard or last_chunk):
                    dve.wait_ge(x_loaded[par], (c - par) * 8 + 32)
                finish(c, par, QG)
                if not (first_guard or last_chunk):
                    statistics(c + 2)

            dve.wait_ge(x_loaded[1], 16)
            statistics(1)
            chunk(0, 0, first_chunk=True)
            chunk(1, 1)
            with dve.Fori(1, NG // 2 - 1) as it:
                chunk(2 * it, 0)
                chunk(2 * it + 1, 1)
            chunk(NG - 2, 0, first_guard=True)
            chunk(NG - 1, 1, last_chunk=True)
            guard_sums(1)
            guard_products(1)
            guard_value(1)
            dve.wait_ge(bound_all, 1)
            dve.tensor_reduce(widest[:, :], range_all[:, :], AX.X, ALU.max).then_inc(gd, 1)
            dve.wait_ge(gd, BATCH * GUARD_STEPS + 1)
            dve.tensor_scalar(wide[:, :], widest[:, :], GUARD_LIMIT, None, ALU.is_gt).then_inc(wide_ready, 1)
            fill_guard_rows(1)
            dve.wait_ge(wide_ready, 1)
            bound_too_wide = dve.value_load(wide[0:1, 0:1], min_val=0, max_val=1)
            with dve.If(bound_too_wide):
                with dve.Fori(0, NG * HEADS) as n:
                    for u in range(QG * TPC):
                        dve.wait_ge(gm_scores, n * (QG * TPC) + u + 1)
                        dve.tensor_reduce(row_max[:, u:u + 1], ps[:, 0:CPB, :], AX.XY, ALU.max).then_inc(gm_scores_used, 1)
                    dve.wait_ge(gm_turned, n + 1)
                    turned = ps[0:QG * TPC, 6, 0:P]
                    dve.tensor_scalar(gm_parts[:, 0, :], turned, -1.0, None, ALU.mult).then_inc(gm_step, 1)
                    dve.wait_ge(gm_step, n * 3 + 1)
                    dve.scalar_tensor_tensor(gm_rest[:, :], turned, -1.0, gm_parts[:, 0, :], ALU.mult, ALU.subtract)\
                        .then_inc(gm_step, 1)
                    dve.wait_ge(gm_step, n * 3 + 2)
                    dve.tensor_copy(gm_parts[:, 1, :], gm_rest[:, :]).then_inc(gm_step, 1)
                    dve.wait_ge(gm_step, n * 3 + 3)
                    dve.tensor_tensor(gm_parts[:, 2, :], gm_rest[:, :], gm_parts[:, 1, :], ALU.subtract).then_inc(gm_split, 1)
                dve.wait_ge(gm_stored, 16 * (NG * HEADS + 1))

            for q in range(QG):
                for half_q in range(2):
                    k = (NG - 1) * QG + 2 * q + half_q
                    dve.wait_ge(am_ready, k + 1)
                    dve.reciprocal(rnorm[:, 0, :], last_am[:, :, KV]).then_inc(rnorm_ready, 1)
                    dve.wait_ge(rnorm_ready, k + 1)
                    for t in range(2):
                        row = resid[:, NT - TPC + 2 * half_q + t, q * KV:q * KV + KV]
                        last = dve.scalar_tensor_tensor(row, last_am[:, t, 0:KV], rnorm[:, 0, t:t + 1], row, ALU.mult, ALU.add)
                    last.then_inc(am_used, 1)

            dve.wait_ge(w8_loaded, 16)
            mag, sign, twice = work[:, 0:4, :], work[:, 4:8, :], y_out[:, :, :]
            dve.tensor_copy(mag, w8[:, :, :].bitcast(U8)).then_inc(dec, 1)
            dve.wait_ge(dec, 1)
            dve.tensor_scalar(sign, mag, 128.0, 128.0, ALU.is_ge, ALU.mult).then_inc(dec, 1)
            dve.wait_ge(dec, 2)
            dve.tensor_tensor(mag, mag, sign, ALU.subtract).then_inc(dec, 1)
            dve.wait_ge(dec, 3)
            dve.tensor_scalar(mag.bitcast(I32), mag, 960.0, 2.0 ** 20, ALU.add, ALU.mult).then_inc(dec, 1)
            dve.wait_ge(dec, 4)
            dve.tensor_scalar(twice, mag, 2.0, -2.0 ** -6, ALU.mult, ALU.add).then_inc(dec, 1)
            dve.wait_ge(dec, 5)
            dve.tensor_tensor(mag, mag, twice, ALU.min).then_inc(dec, 1)
            dve.tensor_scalar(sign, sign, -2.0 / 128.0, 1.0, ALU.mult, ALU.add).then_inc(dec, 1)
            dve.wait_ge(dec, 7)
            dve.tensor_tensor(w_val[:, :, :], mag, sign, ALU.mult).then_inc(dec, 1)

            def copy_ffn_weight():
                for k in range(KT):
                    dve.wait_ge(wf_turned, k + 1)
                    dve.tensor_copy(wT_ffn[:, k, :], ffn_tp).then_inc(wf_copied, 1)

            def add_head(n, par, g, h):
                dve.wait_ge(pv_done, n * ST + ST)
                dve.transpose(by_token[:, :, :, :].rearrange("p q t v -> p (q t v)"), acc[par]).then_inc(acc_read, 1)
                dve.wait_ge(acc_read, n + 1 + TWO_FREE)
                dve.reciprocal(rden[:, :, :], by_token[:, :, :, DH]).then_inc(rden_ready, 1)
                dve.wait_ge(rden_ready, n + 1)
                dve.tensor_tensor(head_out[:, :, :, :], by_token[:, :, :, 0:DH],
                                  rden[:, :, :].unsqueeze(3).to_broadcast([P, QG, TPC, DH]), ALU.mult)\
                    .then_inc(head_out_ready, 1)
                dve.wait_ge(head_out_ready, n + 1)
                cols = resid[:, bass.ds(g * TPC, TPC), :].rearrange("p t (q f) -> p q t f", q=QG)[:, :, :, bass.ds(h * DH, DH)]
                dve.tensor_tensor(cols, cols, head_out[:, :, :, :], ALU.add)

            def chunk_moments(g):
                dve.drain()
                for t in range(TPC):
                    dve.bn_stats(stats[:, t, :], resid[:, bass.ds(g * TPC + t, 1), :].rearrange("p a d -> p (a d)"))
                dve.drain()
                for t in range(TPC):
                    last = dve.bn_aggr(moments[:, 0, t, :], stats[:, t, :])
                last.then_inc(f_moments, 1)
                dve.wait_ge(f_rstd, g + 1)
                dve.tensor_scalar(rstd_s[:, :], rstd[:, 0, :], inv_s, None, ALU.mult).then_inc(f_step, 1)
                dve.wait_ge(f_step, g * 6 + 1)

            def round_to_float8(g):
                chunk_moments(g)
                xs, big = work[:, 0:4, :], work[:, 4:8, :]
                for t in range(TPC):
                    last = dve.tensor_scalar(work[:, t, :], resid[:, bass.ds(g * TPC + t, 1), :].rearrange("p a d -> p (a d)"),
                                             moments[:, 0, t, 0:1], rstd_s[:, t:t + 1], ALU.subtract, ALU.mult)
                last.then_inc(f_step, 1)
                dve.wait_ge(f_step, g * 6 + 2)
                dve.tensor_scalar(xs, xs, FP8_MAX, -FP8_MAX, ALU.min, ALU.max).then_inc(f_step, 1)
                dve.wait_ge(f_step, g * 6 + 3)
                dve.tensor_scalar(big.bitcast(I32), xs.bitcast(I32), 0x7F800000, None, ALU.bitwise_and).then_inc(f_step, 1)
                dve.wait_ge(f_step, g * 6 + 4)
                dve.tensor_scalar(big, big, 2.0 ** -6, 1.5 * 2.0 ** 20, ALU.max, ALU.mult).then_inc(f_step, 1)
                dve.wait_ge(f_step, g * 6 + 5)
                dve.tensor_tensor(xs, xs, big, ALU.add).then_inc(f_step, 1)
                dve.wait_ge(f_step, g * 6 + 6)
                dve.tensor_tensor(xq, xs, big, ALU.subtract).then_inc(xq_ready, 1)

            def ffn_out(g, t):
                dve.wait_ge(xq_turned, g * TPC + t + 1)
                dve.tensor_copy(xqT[:, :, :].rearrange("p k s -> p (k s)"), ffn_tp).then_inc(xqT_ready, 1)
                dve.wait_ge(ffn_ready, g * TPC + t + 1)
                dve.wait_ge(y_stored, g * 16 + 16)
                dve.scalar_tensor_tensor(y_out[:, bass.ds(t, 1), :].rearrange("p a d -> p (a d)"), ffn_ps, sw,
                                         resid[:, bass.ds(g * TPC + t, 1), :].rearrange("p a d -> p (a d)"),
                                         ALU.mult, ALU.add).then_inc(y_ready, 1)

            def round_last_chunk(t0):
                g = NG - 1
                for stage in range(6):
                    for t in (t0, t0 + 1):
                        done = 5 * t0 + 2 * stage + t - t0
                        if stage > 0:
                            dve.wait_ge(last_step, done - 1)
                        x_s, big = work[:, t, :], work[:, 4 + t, :]
                        if stage == 0:
                            op = dve.tensor_scalar(x_s, resid[:, g * TPC + t, :], moments[:, 0, t, 0:1], rstd_s[:, t:t + 1],
                                                   ALU.subtract, ALU.mult)
                        elif stage == 1:
                            op = dve.tensor_scalar(x_s, x_s, FP8_MAX, -FP8_MAX, ALU.min, ALU.max)
                        elif stage == 2:
                            op = dve.tensor_scalar(big.bitcast(I32), x_s.bitcast(I32), 0x7F800000, None, ALU.bitwise_and)
                        elif stage == 3:
                            op = dve.tensor_scalar(big, big, 2.0 ** -6, 1.5 * 2.0 ** 20, ALU.max, ALU.mult)
                        elif stage == 4:
                            op = dve.tensor_tensor(x_s, x_s, big, ALU.add)
                        else:
                            op = dve.tensor_tensor(xq[:, t, :], x_s, big, ALU.subtract)
                        op.then_inc(xq_ready if stage == 5 else last_step, 1)

            add_head(0, 0, 0, 0)
            copy_ffn_weight()
            add_head(1, 1, 0, 1)
            with dve.Fori(1, HEADS // 2) as hp:
                for par in range(2):
                    add_head(2 * hp + par, par, 0, 2 * hp + par)
            with dve.Fori(1, NG) as g:
                round_to_float8(g - 1)
                with dve.Fori(0, HEADS // 2) as hp:
                    add_head(g * HEADS + 2 * hp, 0, g, 2 * hp)
                    ffn_out(g - 1, hp)
                    add_head(g * HEADS + 2 * hp + 1, 1, g, 2 * hp + 1)
            chunk_moments(NG - 1)
            for t in range(0, TPC, 2):
                round_last_chunk(t)
            for t in range(TPC):
                dve.wait_ge(ffn_ready, (NG - 1) * TPC + t + 1)
                if t == 0:
                    dve.wait_ge(y_stored, 16 * NG)
                dve.scalar_tensor_tensor(y_out[:, t, :], last_ffn[t], sw, resid[:, NT - TPC + t, :], ALU.mult, ALU.add)\
                    .then_inc(y_ready, 1)


def kernel(L0_attn_x, L0_attn_Wq, L0_attn_Wk, L0_attn_Wv, L0_attn_memory, L0_attn_memory_norm, L0_attn_memory_weight,
           L0_ffn_weight, L0_ffn_weight_scale, L0_ffn_input_scale):
    import concourse.bacc as bacc
    from concourse.bass_utils import run_bass_kernel_spmd

    nc = bacc.Bacc("TRN2", target_bir_lowering=False, num_devices=1)
    inputs = {
        "x": np.ascontiguousarray(L0_attn_x).reshape(BATCH * SEQ, DM),
        "Wq": np.ascontiguousarray(L0_attn_Wq),
        "Wk": np.ascontiguousarray(L0_attn_Wk),
        "Wv": np.ascontiguousarray(L0_attn_Wv),
        "memory": np.ascontiguousarray(L0_attn_memory),
        "memory_norm": np.ascontiguousarray(L0_attn_memory_norm),
        "memory_weight": np.ascontiguousarray(L0_attn_memory_weight),
        "weight": np.ascontiguousarray(L0_ffn_weight),
        "weight_scale": np.ascontiguousarray(L0_ffn_weight_scale).reshape(1),
        "input_scale": np.ascontiguousarray(L0_ffn_input_scale).reshape(1),
    }
    aps = [nc.dram_tensor(f"in_{name}", a.shape, mybir.dt.from_np(a.dtype), kind="ExternalInput").ap()
           for name, a in inputs.items()]
    out = nc.dram_tensor("out", (BATCH * SEQ, DM), F32, kind="ExternalOutput").ap()
    q_aug = nc.dram_tensor("q_aug", (NG * HEADS, ROWS, QG * CH), BF16, kind="Internal").ap()
    k_aug = nc.dram_tensor("k_aug", (NG * HEADS, ROWS, CH), BF16, kind="Internal").ap()
    v_aug = nc.dram_tensor("v_aug", (NG, HEADS, P, TPC * VW), F32, kind="Internal").ap()
    guard = nc.dram_tensor("guard", (NG * HEADS, SPLIT, QG * CH), BF16, kind="Internal").ap()
    attention_ffn(nc, *aps, out, q_aug, k_aug, v_aug, guard)
    r = run_bass_kernel_spmd(nc, [{f"in_{name}": a for name, a in inputs.items()}], core_ids=[0])
    return r.results[0]["out"].reshape(BATCH, SEQ, DM)
```
